# Optimizing a Trainium2 kernel written in Bass

```python
import numpy as np
import jax
import jax.numpy as jnp

def _softmax(x, axis=-1):
    return jax.nn.softmax(x, axis=axis)

def _gelu(x):
    return jax.nn.gelu(x, approximate=True)

def _silu(x):
    return jax.nn.silu(x)

def _sigmoid(x):
    return jax.nn.sigmoid(x)

def _layernorm(x, axis=-1, eps=1e-05):
    m = jnp.mean(x, axis=axis, keepdims=True)
    v = jnp.var(x, axis=axis, keepdims=True)
    return (x - m) / jnp.sqrt(v + eps)

def _scatter_add(tgt, idx, src, axis=0):
    return tgt.at[idx].add(src)

def _segment_sum(src, seg, n):
    return jax.ops.segment_sum(src, seg, n)
kernel_name = 'mk_vit_tower_d1_tok_img2048_r4_2bf0a5'

def setup_inputs(seed: int=0):
    np.random.seed(seed)
    _w = jnp.asarray

    def _rec_inputs():
        import jax
        import jax.numpy as jnp
        _rk = jax.random.key(seed)
        x = -0.00178296 + 0.498989 * jax.random.normal(jax.random.fold_in(_rk, 1), (16, 256, 64, 2), jnp.float32)
        return x
    x = _rec_inputs()

    def _L0_tok_setup():
        import jax, jax.numpy as jnp
        import numpy as np
        H, N, CCH, LLEN = (256, 64, 1, 512)
        key = jax.random.key(seed)
        k1, k2 = jax.random.split(key, 2)
        log_dt = jax.random.uniform(k1, (H,), jnp.float32, float(np.log(0.001)), float(np.log(0.1)))
        C = 0.5 * jax.random.normal(k2, (CCH, H, N, 2), jnp.float32)
        log_w_real = jnp.full((H, N), float(np.log(0.5)), jnp.float32)
        w_imag = jnp.broadcast_to(np.pi * jnp.arange(N, dtype=jnp.float32), (H, N)) + jnp.zeros((H, N), jnp.float32)
        return {'C': C, 'log_dt': log_dt, 'log_w_real': log_w_real, 'w_imag': w_imag, 'L': LLEN}
    _L0_tok_all = _L0_tok_setup()
    _L0_tok_in = {k: v for k, v in _L0_tok_all.items() if k in ('log_dt', 'log_w_real', 'w_imag')}
    del _L0_tok_all

    def _L0_attn_setup():
        import jax, jax.numpy as jnp
        import numpy as np
        DIM = 512
        H = 16
        DH = DIM // H
        LATENT = 128
        D_ROPE = 64
        B, S = (2, 512)
        ROPE_THETA = 10000.0

        def _rope_cos_sin(seq_len, d_rope, dtype=jnp.float32):
            inv_freq = 1.0 / ROPE_THETA ** (jnp.arange(0, d_rope, 2, dtype=jnp.float32) / d_rope)
            freqs = jnp.arange(seq_len, dtype=jnp.float32)[:, None] * inv_freq[None, :]
            emb = jnp.concatenate([freqs, freqs], axis=-1)
            return (jnp.cos(emb).astype(dtype), jnp.sin(emb).astype(dtype))

        def _rotate_half(x):
            x1, x2 = jnp.split(x, 2, axis=-1)
            return jnp.concatenate([-x2, x1], axis=-1)

        def _apply_rope(x, cos, sin):
            return x * cos + _rotate_half(x) * sin
        key = jax.random.key(seed)
        ks = jax.random.split(key, 6)
        std = 0.02
        return {'x': jax.random.normal(ks[0], (B, S, DIM), jnp.float32), 'Wq': jax.random.normal(ks[1], (DIM, H * (DH + D_ROPE)), jnp.float32) * std, 'Wdkv': jax.random.normal(ks[2], (DIM, LATENT), jnp.float32) * std, 'Wkr': jax.random.normal(ks[3], (DIM, D_ROPE), jnp.float32) * std, 'Wukv': jax.random.normal(ks[4], (LATENT, H * 2 * DH), jnp.float32) * std, 'Wo': jax.random.normal(ks[5], (H * DH, DIM), jnp.float32) * std}
    _L0_attn_all = _L0_attn_setup()
    _L0_attn_in = {k: v for k, v in _L0_attn_all.items() if k in ('Wq', 'Wdkv', 'Wkr', 'Wukv', 'Wo')}
    del _L0_attn_all

    def _L0_ffn_setup():
        import jax, jax.numpy as jnp
        import numpy as np
        L, N, E, H, K = (512, 8, 512, 2048, 8)
        key = jax.random.key(seed)
        ks = jax.random.split(key, 6)
        return {'x': jax.random.normal(ks[0], (L, N, E), dtype=jnp.float32), 'proj1': jax.random.normal(ks[1], (H, E), dtype=jnp.float32) * 0.02, 'proj1_bias': jax.random.normal(ks[2], (H,), dtype=jnp.float32) * 0.02, 'proj2': jax.random.normal(ks[3], (E, H), dtype=jnp.float32) * 0.02, 'proj2_bias': jax.random.normal(ks[4], (E,), dtype=jnp.float32) * 0.02, 'gate_w': jax.random.normal(ks[5], (E, K), dtype=jnp.float32)}
    _L0_ffn_all = _L0_ffn_setup()
    _L0_ffn_in = {k: v for k, v in _L0_ffn_all.items() if k in ('proj1', 'proj1_bias', 'proj2', 'proj2_bias', 'gate_w')}
    del _L0_ffn_all
    return {'x': x, 'L0_tok_log_dt': _L0_tok_in['log_dt'], 'L0_tok_log_w_real': _L0_tok_in['log_w_real'], 'L0_tok_w_imag': _L0_tok_in['w_imag'], 'L0_attn_Wq': _L0_attn_in['Wq'], 'L0_attn_Wdkv': _L0_attn_in['Wdkv'], 'L0_attn_Wkr': _L0_attn_in['Wkr'], 'L0_attn_Wukv': _L0_attn_in['Wukv'], 'L0_attn_Wo': _L0_attn_in['Wo'], 'L0_ffn_proj1': _L0_ffn_in['proj1'], 'L0_ffn_proj1_bias': _L0_ffn_in['proj1_bias'], 'L0_ffn_proj2': _L0_ffn_in['proj2'], 'L0_ffn_proj2_bias': _L0_ffn_in['proj2_bias'], 'L0_ffn_gate_w': _L0_ffn_in['gate_w']}

def reference(x, L0_tok_log_dt, L0_tok_log_w_real, L0_tok_w_imag, L0_attn_Wq, L0_attn_Wdkv, L0_attn_Wkr, L0_attn_Wukv, L0_attn_Wo, L0_ffn_proj1, L0_ffn_proj1_bias, L0_ffn_proj2, L0_ffn_proj2_bias, L0_ffn_gate_w):
    import jax
    import jax.numpy as jnp

    def _L0_tok_ref(C, log_dt, log_w_real, w_imag, L):
        import jax, jax.numpy as jnp
        import numpy as np
        H, N, CCH, LLEN = (256, 64, 1, 512)
        dt = jnp.exp(log_dt)
        Cc = C[..., 0] + 1j * C[..., 1]
        w = -jnp.exp(log_w_real) + 1j * w_imag
        dtA = w * dt[:, None]
        K = dtA[:, :, None] * jnp.arange(L)
        Cm = Cc * (jnp.exp(dtA) - 1.0) / w
        K = jnp.einsum('chn,hnl->chl', Cm, jnp.exp(K))
        return 2 * K.real

    def _L0_attn_ref(x, Wq, Wdkv, Wkr, Wukv, Wo):
        import jax, jax.numpy as jnp
        import numpy as np
        DIM = 512
        H = 16
        DH = DIM // H
        LATENT = 128
        D_ROPE = 64
        B, S = (2, 512)
        ROPE_THETA = 10000.0

        def _rope_cos_sin(seq_len, d_rope, dtype=jnp.float32):
            inv_freq = 1.0 / ROPE_THETA ** (jnp.arange(0, d_rope, 2, dtype=jnp.float32) / d_rope)
            freqs = jnp.arange(seq_len, dtype=jnp.float32)[:, None] * inv_freq[None, :]
            emb = jnp.concatenate([freqs, freqs], axis=-1)
            return (jnp.cos(emb).astype(dtype), jnp.sin(emb).astype(dtype))

        def _rotate_half(x):
            x1, x2 = jnp.split(x, 2, axis=-1)
            return jnp.concatenate([-x2, x1], axis=-1)

        def _apply_rope(x, cos, sin):
            return x * cos + _rotate_half(x) * sin
        Bd, Sd, _ = x.shape
        q = (x @ Wq).reshape(Bd, Sd, H, DH + D_ROPE)
        q_nope, q_rope = (q[..., :DH], q[..., DH:])
        c_kv = x @ Wdkv
        kv = (c_kv @ Wukv).reshape(Bd, Sd, H, 2 * DH)
        k_nope, v = (kv[..., :DH], kv[..., DH:])
        k_rope = x @ Wkr
        cos, sin = _rope_cos_sin(Sd, D_ROPE, x.dtype)
        q_rope = _apply_rope(q_rope, cos[None, :, None, :], sin[None, :, None, :])
        k_rope = _apply_rope(k_rope, cos[None, :, :], sin[None, :, :])
        scale = 1.0 / jnp.sqrt(jnp.asarray(DH + D_ROPE, x.dtype))
        scores = jnp.einsum('bqhd,bkhd->bhqk', q_nope, k_nope)
        scores = scores + jnp.einsum('bqhd,bkd->bhqk', q_rope, k_rope)
        scores = scores * scale
        causal = jnp.tril(jnp.ones((Sd, Sd), dtype=bool))
        scores = jnp.where(causal[None, None, :, :], scores, jnp.asarray(-1000000000.0, x.dtype))
        attn = jax.nn.softmax(scores, axis=-1)
        out = jnp.einsum('bhqk,bkhd->bqhd', attn, v).reshape(Bd, Sd, H * DH)
        return out @ Wo

    def _L0_ffn_ref(x, proj1, proj1_bias, proj2, proj2_bias, gate_w):
        import jax, jax.numpy as jnp
        import numpy as np
        L, N, E, H, K = (512, 8, 512, 2048, 8)
        dst = jnp.argmax(jnp.einsum('lne,ek->lnk', x, gate_w), axis=-1)
        h = jax.nn.gelu(jnp.einsum('lne,he->lnh', x, proj1) + proj1_bias, approximate=False)
        out = jnp.einsum('lnh,eh->lne', h, proj2) + proj2_bias
        del dst
        return out
    h = _L0_tok_ref(x, L0_tok_log_dt, L0_tok_log_w_real, L0_tok_w_imag, 512)
    h = h + _L0_attn_ref(_layernorm(h, axis=-1), L0_attn_Wq, L0_attn_Wdkv, L0_attn_Wkr, L0_attn_Wukv, L0_attn_Wo)
    h = h + _L0_ffn_ref(_layernorm(h, axis=-1), L0_ffn_proj1, L0_ffn_proj1_bias, L0_ffn_proj2, L0_ffn_proj2_bias, L0_ffn_gate_w)
    return h

_drawn_inputs = setup_inputs


def setup_inputs(seed=0):
    import zlib

    import numpy as np

    out = dict(_drawn_inputs(seed))
    spreads = {'L0_tok_log_w_real': (-0.6931471824645996, 0.2)}
    factors = {}
    for name, (base, spread) in spreads.items():
        noise = np.random.default_rng([zlib.crc32(name.encode()), seed]).standard_normal(out[name].shape)
        drawn = base * np.exp(spread * noise) if base else spread * noise
        out[name] = jnp.asarray(drawn.astype(out[name].dtype))
    for name, factor in factors.items():
        out[name] = (out[name] * factor).astype(out[name].dtype)
    return out
```

```python
from contextlib import ExitStack

import concourse.bass as bass
from concourse import mybir

F32 = mybir.dt.float32
F32R = mybir.dt.float32r
I32 = mybir.dt.int32
ALU = mybir.AluOpType
ACT = mybir.ActivationFunctionType

P = 128
BATCH, SEQ, DIM = 16, 256, 512
MODES = 64
TOKENS = BATCH * SEQ
HEADS, DH, ROPE, LATENT = 16, 32, 64, 128
DQK = DH + ROPE
HIDDEN = 2048
KD = DIM // P
TT = SEQ // P
EPS = 1e-5
SCALE = 1.0 / (DQK ** 0.5)
MASKED = -1e10

WQ, WDKV, WKR = 0, KD * HEADS * DQK, KD * (HEADS * DQK + LATENT)
WUK = WKR + KD * 2 * ROPE
WUV = WUK + HEADS * DH
WO = WUV + HEADS * DH
WCOLS = WO + KD * DIM
WCHUNK = 2048

NA, NI, NJ = 8, 8, 8
HC = 128
HB = 8

MAGIC = 1.5 * 2.0 ** 23
LOG2E, LN2_HI, LN2_LO = 1.4426950408889634, 0.693359375, -2.12194440054690583e-4
PI = 3.141592653589793
C1 = 6.28125
C2 = 0.0019350051879882812
C3 = 2 * PI - C1 - C2
PI_BELOW = 3.1415925


def dve_chain(dve, sem):
    count = [0]

    def link(ins):
        count[0] += 1
        ins.then_inc(sem, 1)
        dve.wait_ge(sem, count[0])

    return link


def token_mixer(nc, c_parts, log_dt, log_w_real, w_imag, weights, whi, wlo, ident, mixed):
    with ExitStack() as ctx:
        def sb(name, shape, dt=F32):
            return ctx.enter_context(nc.sbuf_tensor(name, shape, dt))

        def sem(name):
            return ctx.enter_context(nc.semaphore(name))

        logs = sb("logs", [P, 2, SEQ])
        wim = sb("wim", [P, SEQ])
        ck = sb("ck", [P, 2 * SEQ])
        cr = sb("cr", [P, 2 * SEQ])
        cp = sb("cp", [P, 2 * SEQ])
        dtw = sb("dtw", [P, 2, SEQ])
        dre = sb("dre", [P, SEQ])
        dim = sb("dim", [P, SEQ])
        half_pi = sb("half_pi", [P, 1])
        cbuf = sb("cbuf", [P, 2, HC, BATCH])
        pre = sb("pre", [P, NI, HC])
        pim = sb("pim", [P, NI, HC])
        vj_a = sb("vj_a", [P, NJ, HC])
        vj_b = sb("vj_b", [P, NJ, HC])
        za_a = sb("za_a", [P, NA, HC])
        za_b = sb("za_b", [P, NA, HC])
        ang = sb("ang", [P, 8, HC])
        kbuf = sb("kbuf", [P, 8, HC])
        ebuf = sb("ebuf", [P, 8, HC])
        re_t = sb("re_t", [P, 8, HC])
        im_t = sb("im_t", [P, 8, HC])
        gt = sb("gt", [P, 10, HC])
        v_t1 = sb("v_t1", [P, 2, HB, NI * NJ])
        v_t2 = sb("v_t2", [P, 2, HB, NI * NJ])
        vblk = sb("vblk", [P, 2, HB, NI * NJ])
        w1 = sb("w1", [P, 2, HB, BATCH * NA])
        w2 = sb("w2", [P, 2, HB, BATCH * NA])
        ystage = sb("ystage", [P, 2, HB * NI * NJ])
        wraw = sb("wraw", [P, 2, WCHUNK])
        ypsum = [ctx.enter_context(nc.psum_tensor(f"ypsum{i}", [P, HB * NI * NJ], F32)) for i in range(2)]

        params_in, c_in, chain, consts_ready, ident_ready = map(
            sem, ("params_in", "c_in", "chain", "consts_ready", "ident_ready"))
        wraw_in = [sem(f"wraw_in{i}") for i in range(2)]
        whi_ready, wlo_ready = sem("whi_ready"), sem("wlo_ready")
        angle_ready, exps_ready, abs_ready, sin_ready, cos_ready, half_ready, tanh_ready = map(
            sem, ("angle_ready", "exps_ready", "abs_ready", "sin_ready", "cos_ready", "half_ready", "tanh_ready"))
        group_read, tables_ready, c_used = map(sem, ("group_read", "tables_ready", "c_used"))
        vt1_ready, vt2_ready, v_ready, w1_ready, w2_pool, w2_dve = map(
            sem, ("vt1_ready", "vt2_ready", "v_ready", "w1_ready", "w2_pool", "w2_dve"))
        block_done, y_out, gate_sp = map(sem, ("block_done", "y_out", "gate_sp"))
        y_stored = [sem(f"y_stored{i}") for i in range(2)]

        NCH = SEQ // HC
        NB = HC // HB
        NW = WCOLS // WCHUNK
        GROUPS = ((1, "p"), (0, "j"), (2, "a"))
        EXPS = {"p": [NJ * i for i in range(NI)], "j": list(range(NJ)), "a": [NI * NJ * a for a in range(NA)]}
        block = ctx.enter_context(nc.Block())

        @block.sync
        def _(sp):
            sp.dma_start(logs[:, 0, :], log_dt.rearrange("(a h) -> a h", a=1).to_broadcast([P, SEQ])).then_inc(params_in, 16)
            for half in range(2):
                rows = slice(half * MODES, (half + 1) * MODES)
                sp.dma_start(logs[rows, 1, :], log_w_real).then_inc(params_in, 16)
                sp.dma_start(wim[rows, :], w_imag).then_inc(params_in, 16)
            for chunk in range(NCH):
                if chunk:
                    sp.wait_ge(c_used, chunk)
                for half in range(2):
                    sp.dma_start(cbuf[half * MODES:(half + 1) * MODES, :, :, :],
                                 c_parts[:, :, chunk * HC:(chunk + 1) * HC, :].rearrange("r n h c -> n r h c")
                                 ).then_inc(c_in, 16)
                with sp.Fori(0, NB // 2) as i:
                    for p in range(2):
                        n = i * 2 + (chunk * NB + p)
                        sp.wait_ge(y_out, n + 1)
                        sp.sem_inc(gate_sp, 1)
                        sp.dma_start(mixed[:, bass.ds(i * (2 * HB) + (chunk * HC + p * HB), HB), :],
                                     ystage[:, p, :].rearrange("q (h l) -> q h l", h=HB)).then_inc(y_stored[p], 16)
            for p in range(2):
                sp.wait_ge(y_stored[p], 8 * NCH * NB)

        @block.gpsimd
        def _(pool):
            pool.memset(half_pi[:], PI / 2).then_inc(consts_ready, 1)
            pool.memset(ident[:], 0.0).then_inc(ident_ready, 1)
            pool.wait_ge(ident_ready, 1)
            pool.affine_select(out=ident[:], in_=ident[:], compare_op=ALU.not_equal, fill=1.0, base=0,
                               pattern=[[-1, P]], channel_multiplier=1).then_inc(ident_ready, 1)

            for n in range(NW):
                cols = slice(n * WCHUNK, (n + 1) * WCHUNK)
                pool.wait_ge(whi_ready, n + 1)
                pool.tensor_tensor(wlo[:, cols], wraw[:, n % 2, :], whi[:, cols].bitcast(F32),
                                   ALU.subtract).then_inc(wlo_ready, 1)

            for chunk in range(NCH):
                pool.wait_ge(tables_ready, chunk + 1)
                pool.wait_ge(c_in, 32 * (chunk + 1))
                with pool.Fori(0, NB // 2) as i:
                    for p in range(2):
                        n = i * 2 + (chunk * NB + p)
                        h0 = i * (2 * HB) + p * HB
                        pool.wait_ge(block_done, n + 1)
                        pool.wait_ge(v_ready, n)
                        pool.tensor_tensor(
                            v_t2[:, p].rearrange("q h (i j) -> q h i j", i=NI),
                            pim[:, :, bass.ds(h0, HB)].rearrange("q i h -> q h i").unsqueeze(3).to_broadcast([P, HB, NI, NJ]),
                            vj_b[:, :, bass.ds(h0, HB)].rearrange("q j h -> q h j").unsqueeze(2).to_broadcast([P, HB, NI, NJ]),
                            ALU.mult).then_inc(vt2_ready, 1)
                        pool.tensor_tensor(
                            w2[:, p, 0:HB // 2].rearrange("q h (c a) -> q h c a", c=BATCH),
                            cbuf[:, 1, bass.ds(h0, HB // 2), :].unsqueeze(3).to_broadcast([P, HB // 2, BATCH, NA]),
                            za_b[:, :, bass.ds(h0, HB // 2)].rearrange("q a h -> q h a").unsqueeze(2).to_broadcast([P, HB // 2, BATCH, NA]),
                            ALU.mult).then_inc(w2_pool, 1)

        @block.scalar
        def _(act):
            def split_weights(n):
                cols = slice(n * WCHUNK, (n + 1) * WCHUNK)
                act.wait_ge(wraw_in[n % 2], 16 * (n // 2 + 1))
                act.activation(whi[:, cols], wraw[:, n % 2, :], ACT.Copy).then_inc(whi_ready, 1)

            def load_weights(n):
                if n >= 2:
                    act.wait_ge(wlo_ready, n - 1)
                act.dma_start(wraw[:, n % 2, :], weights[:, n * WCHUNK:(n + 1) * WCHUNK]).then_inc(wraw_in[n % 2], 16)

            load_weights(0)
            load_weights(1)
            act.wait_ge(consts_ready, 1)
            groups = 0
            for chunk in range(NCH):
                for _, name in GROUPS:
                    groups += 1
                    re, im = (pre, pim) if name == "p" else (re_t, im_t)
                    act.wait_ge(angle_ready, groups)
                    act.activation(im[:], ang[:], ACT.Sin).then_inc(sin_ready, 1)
                    act.wait_ge(abs_ready, groups)
                    act.activation(re[:], kbuf[:], ACT.Sin, scale=-1.0, bias=half_pi[:, 0:1]).then_inc(cos_ready, 1)
                    if name == "j":
                        act.activation(gt[:, 0, :], ang[:, 1, :], ACT.Sin, scale=0.5).then_inc(half_ready, 1)
                    act.activation(ebuf[:], ebuf[:], ACT.Exp).then_inc(exps_ready, 1)
                    if name == "j":
                        act.activation(gt[:, 1, :], dre[:, chunk * HC:(chunk + 1) * HC], ACT.Tanh,
                                       scale=0.5).then_inc(tanh_ready, 1)
                    if chunk == 0:
                        split_weights(groups - 1)
                        if groups - 1 + 2 < NW:
                            load_weights(groups - 1 + 2)
                if chunk == 0:
                    for n in range(len(GROUPS), NW):
                        split_weights(n)
                with act.Fori(0, NB // 2) as i:
                    for p in range(2):
                        n = i * 2 + (chunk * NB + p)
                        act.wait_ge(block_done, n + 3)
                        act.wait_ge(y_stored[p], i * 16 + chunk * NB * 8)
                        act.activation(ystage[:, p, :], ypsum[p][:], ACT.Copy).then_inc(y_out, 1)

        @block.vector
        def _(dve):
            link = dve_chain(dve, chain)
            dve.wait_ge(params_in, 16 * 5)
            x = logs[:].rearrange("q r h -> q (r h)")
            link(dve.tensor_scalar(ck[:], x, LOG2E, MAGIC, ALU.mult, ALU.add))
            link(dve.tensor_scalar(ck[:], ck[:], MAGIC, None, ALU.subtract))
            link(dve.tensor_scalar(ck[:], ck[:], -126.0, 127.0, ALU.max, ALU.min))
            link(dve.scalar_tensor_tensor(out=cr[:], in0=ck[:], scalar=-LN2_HI, in1=x, op0=ALU.mult, op1=ALU.add))
            link(dve.scalar_tensor_tensor(out=cr[:], in0=ck[:], scalar=-LN2_LO, in1=cr[:], op0=ALU.mult, op1=ALU.add))
            factors = [1 / 5040, 1 / 720, 1 / 120, 1 / 24, 1 / 6, 1 / 2, 1.0]
            link(dve.tensor_scalar(cp[:], cr[:], factors[0], None, ALU.mult))
            for f in factors[1:]:
                link(dve.scalar_tensor_tensor(out=cp[:], in0=cp[:], scalar=f, in1=cr[:], op0=ALU.add, op1=ALU.mult))
            link(dve.tensor_scalar(cp[:], cp[:], 1.0, None, ALU.add))
            ci = ck[:].bitcast(I32)
            link(dve.tensor_scalar(ci, ck[:], 127.0, 2.0 ** 23, ALU.add, ALU.mult))
            link(dve.tensor_tensor(dtw[:].rearrange("q r h -> q (r h)"), cp[:], ck[:], ALU.mult))
            link(dve.scalar_tensor_tensor(out=dre[:], in0=dtw[:, 1, :], scalar=-1.0, in1=dtw[:, 0, :],
                                          op0=ALU.mult, op1=ALU.mult))
            link(dve.tensor_tensor(dim[:], wim[:], dtw[:, 0, :], ALU.mult))

            groups = 0
            for chunk in range(NCH):
                hs = slice(chunk * HC, (chunk + 1) * HC)
                if chunk:
                    dve.wait_ge(w2_pool, chunk * NB)
                for _, name in GROUPS:
                    groups += 1
                    re, im = (pre, pim) if name == "p" else (re_t, im_t)
                    for e, power in enumerate(EXPS[name]):
                        dve.tensor_scalar(ang[:, e, :], dim[:, hs], float(power), None, ALU.mult)
                        last = dve.tensor_scalar(ebuf[:, e, :], dre[:, hs], float(power), None, ALU.mult)
                    link(last)
                    link(dve.tensor_scalar(kbuf[:], ang[:], 1 / (2 * PI), MAGIC, ALU.mult, ALU.add))
                    link(dve.tensor_scalar(kbuf[:], kbuf[:], MAGIC, None, ALU.subtract))
                    for c in (C1, C2, C3):
                        link(dve.scalar_tensor_tensor(out=ang[:], in0=kbuf[:], scalar=-c, in1=ang[:],
                                                      op0=ALU.mult, op1=ALU.add))
                    dve.tensor_scalar(ang[:], ang[:], PI_BELOW, -PI_BELOW, ALU.min, ALU.max).then_inc(angle_ready, 1)
                    dve.wait_ge(angle_ready, groups)
                    dve.scalar_tensor_tensor(out=kbuf[:], in0=ang[:], scalar=-1.0, in1=ang[:],
                                             op0=ALU.mult, op1=ALU.max).then_inc(abs_ready, 1)
                    dve.wait_ge(exps_ready, groups)
                    dve.wait_ge(sin_ready, groups)
                    dve.wait_ge(cos_ready, groups)
                    if name == "j":
                        link(dve.tensor_copy(gt[:, 2, :], re[:, 1, :]))
                    link(dve.tensor_tensor(re[:], re[:], ebuf[:], ALU.mult))
                    link(dve.tensor_tensor(im[:], im[:], ebuf[:], ALU.mult))
                    lo, up = slice(0, MODES), slice(MODES, P)
                    if name == "j":
                        dve.tensor_copy(vj_a[lo], re[lo])
                        dve.tensor_copy(vj_a[up], im[up])
                        dve.tensor_scalar(vj_b[lo], im[lo], -1.0, None, ALU.mult)
                        link(dve.tensor_copy(vj_b[up], re[up]))
                        dve.wait_ge(half_ready, chunk + 1)
                        dve.wait_ge(tanh_ready, chunk + 1)
                        g = [gt[:, k, :] for k in range(10)]
                        wr, wi = dtw[:, 1, hs], wim[:, hs]
                        link(dve.tensor_scalar(g[3], g[1], -1.0, 1.0, ALU.mult, ALU.add))
                        link(dve.reciprocal(g[4], g[3]))
                        link(dve.scalar_tensor_tensor(out=g[3], in0=g[1], scalar=2.0, in1=g[4], op0=ALU.mult, op1=ALU.mult))
                        link(dve.tensor_tensor(g[3], g[3], g[2], ALU.mult))
                        link(dve.tensor_tensor(g[4], g[0], g[0], ALU.mult))
                        link(dve.scalar_tensor_tensor(out=g[3], in0=g[4], scalar=-2.0, in1=g[3], op0=ALU.mult, op1=ALU.add))
                        link(dve.tensor_copy(g[4], im[:, 1, :]))
                        link(dve.tensor_tensor(g[5], wr, wr, ALU.mult))
                        link(dve.tensor_tensor(g[6], wi, wi, ALU.mult))
                        link(dve.tensor_tensor(g[5], g[5], g[6], ALU.add))
                        link(dve.reciprocal(g[6], g[5]))
                        link(dve.tensor_scalar(g[6], g[6], 2.0, None, ALU.mult))
                        link(dve.tensor_tensor(g[7], g[4], wi, ALU.mult))
                        link(dve.tensor_tensor(g[5], g[3], wr, ALU.mult))
                        link(dve.tensor_tensor(g[7], g[7], g[5], ALU.subtract))
                        link(dve.tensor_tensor(g[8], g[7], g[6], ALU.mult))
                        link(dve.tensor_tensor(g[7], g[4], wr, ALU.mult))
                        link(dve.tensor_tensor(g[5], g[3], wi, ALU.mult))
                        link(dve.tensor_tensor(g[7], g[7], g[5], ALU.add))
                        link(dve.scalar_tensor_tensor(out=g[9], in0=g[7], scalar=-1.0, in1=g[6], op0=ALU.mult, op1=ALU.mult))
                    if name == "a":
                        g_re = gt[:, 8:9, :].to_broadcast([P, NA, HC])
                        g_im = gt[:, 9:10, :].to_broadcast([P, NA, HC])
                        link(dve.tensor_tensor(ang[:], re[:], g_re, ALU.mult))
                        link(dve.tensor_tensor(kbuf[:], im[:], g_im, ALU.mult))
                        link(dve.tensor_tensor(ang[:], ang[:], kbuf[:], ALU.subtract))
                        link(dve.tensor_tensor(kbuf[:], re[:], g_im, ALU.mult))
                        link(dve.tensor_tensor(ebuf[:], im[:], g_re, ALU.mult))
                        link(dve.tensor_tensor(kbuf[:], kbuf[:], ebuf[:], ALU.add))
                        dve.tensor_copy(za_a[lo], ang[lo])
                        dve.tensor_scalar(za_a[up], kbuf[up], -1.0, None, ALU.mult)
                        dve.tensor_scalar(za_b[lo], kbuf[lo], -1.0, None, ALU.mult)
                        dve.tensor_scalar(za_b[up], ang[up], -1.0, None, ALU.mult).then_inc(tables_ready, 1)
                dve.wait_ge(tables_ready, chunk + 1)
                dve.wait_ge(c_in, 32 * (chunk + 1))
                if chunk == 0:
                    dve.sem_inc(block_done, 2)
                with dve.Fori(0, NB // 2) as i:
                    for p in range(2):
                        n = i * 2 + (chunk * NB + p)
                        h0 = i * (2 * HB) + p * HB
                        dve.wait_ge(block_done, n + 1)
                        dve.tensor_tensor(
                            v_t1[:, p].rearrange("q h (i j) -> q h i j", i=NI),
                            pre[:, :, bass.ds(h0, HB)].rearrange("q i h -> q h i").unsqueeze(3).to_broadcast([P, HB, NI, NJ]),
                            vj_a[:, :, bass.ds(h0, HB)].rearrange("q j h -> q h j").unsqueeze(2).to_broadcast([P, HB, NI, NJ]),
                            ALU.mult).then_inc(vt1_ready, 1)
                        dve.tensor_tensor(
                            w1[:, p].rearrange("q h (c a) -> q h c a", c=BATCH),
                            cbuf[:, 0, bass.ds(h0, HB), :].unsqueeze(3).to_broadcast([P, HB, BATCH, NA]),
                            za_a[:, :, bass.ds(h0, HB)].rearrange("q a h -> q h a").unsqueeze(2).to_broadcast([P, HB, BATCH, NA]),
                            ALU.mult).then_inc(w1_ready, 1)
                        dve.tensor_tensor(
                            w2[:, p, HB // 2:].rearrange("q h (c a) -> q h c a", c=BATCH),
                            cbuf[:, 1, bass.ds(h0 + HB // 2, HB // 2), :].unsqueeze(3).to_broadcast([P, HB // 2, BATCH, NA]),
                            za_b[:, :, bass.ds(h0 + HB // 2, HB // 2)].rearrange("q a h -> q h a").unsqueeze(2).to_broadcast([P, HB // 2, BATCH, NA]),
                            ALU.mult).then_inc(w2_dve, 1)
                        dve.wait_ge(vt1_ready, n + 1)
                        dve.wait_ge(vt2_ready, n + 1)
                        dve.tensor_tensor(vblk[:, p], v_t1[:, p], v_t2[:, p], ALU.add).then_inc(v_ready, 1)
                dve.wait_ge(w2_dve, (chunk + 1) * NB)
                dve.wait_ge(w2_pool, (chunk + 1) * NB)
                dve.sem_inc(c_used, 1)

        @block.tensor
        def _(pe):
            for chunk in range(NCH):
                with pe.Fori(0, NB // 2) as i:
                    for p in range(2):
                        n = i * 2 + (chunk * NB + p)
                        pe.wait_ge(w1_ready, n + 1)
                        pe.wait_ge(w2_pool, n + 1)
                        pe.wait_ge(w2_dve, n + 1)
                        pe.wait_ge(v_ready, n + 1)
                        pe.wait_ge(y_out, i * 2 + (chunk * NB + p - 1) if chunk or p else i * 2)
                        for h in range(HB):
                            out = ypsum[p][:, h * NI * NJ:(h + 1) * NI * NJ]
                            pe.matmul(out, w1[:, p, h, :], vblk[:, p, h, :], start=True, stop=False)
                            last = pe.matmul(out, w2[:, p, h, :], vblk[:, p, h, :], start=False, stop=True)
                        last.then_inc(block_done, 1)


def attention_order():
    order = []
    fill = {
        0: [("QB", 0, 0)], 1: [("QB", 0, 1)],
        2: [("LOAD", 1, 0), ("LNS", 1, 0)], 3: [("LNR", 1, 0)], 4: [("LNN", 1, 0)],
        6: [("XT", 1, 0), ("XT", 1, 1)], 7: [("CKV", 1, 0)], 8: [("KR", 1, 0)],
        9: [("QN", 1, 0)], 12: [("QN", 1, 1)],
        17: [("KRX", 1, 0)], 18: [("KN", 1, 0)], 19: [("KN", 1, 1)],
    }
    for step in range(HEADS + 5):
        if step % 2 == 0 and step < HEADS:
            order.append(("QT", 0, step // 2))
        if 1 <= step <= HEADS:
            order.append(("S", 0, step - 1))
        if 2 <= step <= HEADS + 1:
            order.append(("REC", 0, step - 2))
        if step >= 8 and (step - 8) % 4 == 0:
            order.append(("PV", 0, (step - 8) // 4))
        if 4 <= step <= HEADS + 3:
            order.append(("PT", 0, step - 4))
        order += fill.get(step, [])
    order += [("V", 1, 0), ("V", 1, 1), ("WO", 0, 0), ("WO", 0, 1), ("LN2S", 0, 0), ("LN2R", 0, 0),
              ("QA", 1, 0), ("LN2N", 0, 0), ("QA", 1, 1), ("X2T", 0, 0), ("X2T", 0, 1)]
    return order


ORDER = attention_order()
FIRST = [("LOAD", 0, 0), ("LNS", 0, 0), ("LNR", 0, 0), ("LNN", 0, 0), ("XT", 0, 0), ("XT", 0, 1), ("CKV", 0, 0),
         ("KR", 0, 0), ("KRX", 0, 0), ("QN", 0, 0), ("QN", 0, 1), ("QA", 0, 0), ("QA", 0, 1),
         ("V", 0, 0), ("V", 0, 1), ("KN", 0, 0), ("KN", 0, 1)]
LAST = [s for s in ORDER if s[1] == 0]
SHARED = ("XT", "CKV", "KR", "QN", "QA", "QB", "KN", "V", "WO", "X2T")


def attention(nc, mixed, whi, wlo, ident, rope_tok, rope_feat, causal, h2_dram, x2_dram):
    with ExitStack() as ctx:
        def sb(name, shape, dt=F32):
            return ctx.enter_context(nc.sbuf_tensor(name, shape, dt))

        def bank(name, shape):
            return ctx.enter_context(nc.psum_tensor(name, shape, F32))

        def sem(name):
            return ctx.enter_context(nc.semaphore(name))

        RING = 6
        mask = sb("mask", [P, 3 * P])
        cos_sin = sb("cos_sin", [P, 2, TT, ROPE])
        cos_sin_t = sb("cos_sin_t", [P, SEQ])
        h_sb = sb("h_sb", [P, 2, TT, DIM])
        xn = [sb(f"xn{j}", [P, TT, DIM]) for j in range(2)]
        stats = [sb(f"stats{j}", [P, TT, 6]) for j in range(2)]
        meanvar = [sb(f"meanvar{j}", [P, TT, 2]) for j in range(2)]
        lnt = [sb(f"lnt{j}", [P, 6, TT]) for j in range(2)]
        xt_hi = sb("xt_hi", [P, KD, SEQ], F32R)
        xt_lo = sb("xt_lo", [P, KD, SEQ], F32R)
        ck_hi = sb("ck_hi", [P, SEQ], F32R)
        ck_lo = sb("ck_lo", [P, SEQ], F32R)
        kr_a = sb("kr_a", [ROPE, SEQ])
        kr_b = sb("kr_b", [ROPE, SEQ])
        kr_s = sb("kr_s", [ROPE, SEQ])
        q_tok = sb("q_tok", [P, 2, TT, HEADS, DQK])
        q_rot = sb("q_rot", [P, 2, 8, ROPE])
        k_t = sb("k_t", [DQK, HEADS, SEQ])
        v_sb = sb("v_sb", [P, 2, TT, HEADS * DH])
        q_t = sb("q_t", [DQK, 2, 2, SEQ])
        probs = sb("probs", [P, RING, 3 * P])
        probs_t = sb("probs_t", [P, RING, 3 * P])
        neg_max = sb("neg_max", [P, HEADS, TT])
        sums = sb("sums", [P, HEADS, TT])
        recips = sb("recips", [P, HEADS, TT])
        o_hi = sb("o_hi", [P, KD, SEQ], F32R)
        o_lo = sb("o_lo", [P, KD, SEQ], F32R)
        x2_t = sb("x2_t", [P, KD, SEQ])

        shared = [bank(f"shared{i}", [P, 512]) for i in range(2)]
        qt_bank = bank("qt_bank", [DQK, 2, SEQ])
        s_bank = [bank(f"s_bank{i}", [P, 3 * P]) for i in range(2)]
        pt_bank = [bank(f"pt_bank{i}", [P, 3 * P]) for i in range(2)]
        pv_bank = bank("pv_bank", [P, SEQ])

        tables_in = sem("tables_in")
        h_in = [sem(f"h_in{i}") for i in range(2)]
        stat_done, var_ready, guess_ready, newton, xn_ready = (
            [sem(f"{n}{j}") for j in range(2)]
            for n in ("stat_done", "var_ready", "guess_ready", "newton", "xn_ready"))
        gates = {e: sem(f"gate_{e}") for e in ("sp", "pool", "dve")}
        done = {k: sem(f"done_{k}") for k in SHARED + ("QT", "S", "PT", "PV")}
        PER = {"XT": 2, "CKV": 1, "KR": 1, "QN": 2, "QA": 2, "QB": 2, "KN": 2, "V": 2, "WO": 2, "X2T": 2,
               "QT": 8, "S": HEADS, "PT": HEADS, "PV": 4}
        xt_hi_ready, xt_lo_ready, ck_hi_ready, ck_lo_ready, kr_read, kr_sum, kr_ready = map(
            sem, ("xt_hi_ready", "xt_lo_ready", "ck_hi_ready", "ck_lo_ready", "kr_read", "kr_sum", "kr_ready"))
        q_nope_ready, rope_read, q_rope_ready, kn_act, kn_dve, v_ready = map(
            sem, ("q_nope_ready", "rope_read", "q_rope_ready", "kn_act", "kn_dve", "v_ready"))
        qt_ready, max_ready, exp_ready, recip_ready, norm_ready, pt_act, pt_dve, o_hi_ready, o_lo_ready = map(
            sem, ("qt_ready", "max_ready", "exp_ready", "recip_ready", "norm_ready", "pt_act", "pt_dve",
                  "o_hi_ready", "o_lo_ready"))
        h2_ready, x2_ready, h2_stored, x2_stored = map(sem, ("h2_ready", "x2_ready", "h2_stored", "x2_stored"))

        def at(b, per, n):
            return b[0] * (2 * per) + (b[1] * per + n)

        def wait(eng, s, b, per, n):
            value = at(b, per, n)
            if not isinstance(value, int) or value > 0:
                eng.wait_ge(s, value)

        FREES = {"XT": [(xt_lo_ready, 2)], "CKV": [(ck_lo_ready, 1)], "KR": [(kr_read, 1)],
                 "QN": [(q_nope_ready, 2)], "QA": [(rope_read, 4)], "QB": [(rope_read, 4)],
                 "KN": [(kn_act, 2), (kn_dve, 2)], "V": [(v_ready, 2)], "WO": [(h2_ready, 2)], "X2T": [(x2_ready, 2)]}
        PT_ACT = [h for h in range(HEADS) if h % 4 == 1]

        def gate(eng, name):
            eng.sem_inc(gates[name], 1)

        def walk(eng, stages):
            stages(FIRST, (0, 0), True)
            with eng.Fori(0, BATCH // 2 - 1) as i:
                stages(ORDER, (i, 0), False)
                stages(ORDER, (i, 1), False)
            stages(ORDER, (BATCH // 2 - 1, 0), False)
            stages(LAST, (BATCH // 2 - 1, 1), False)

        block = ctx.enter_context(nc.Block())

        @block.sync
        def _(sp):
            sp.dma_start(mask[:], causal).then_inc(tables_in, 16)
            sp.dma_start(cos_sin[:], rope_tok).then_inc(tables_in, 16)
            sp.dma_start(cos_sin_t[:], rope_feat).then_inc(tables_in, 16)

            def rows(b, t):
                return bass.ds(b[0] * (2 * SEQ) + (b[1] * SEQ + t * P), P)

            def stages(order, base, first):
                for stage, ahead, n in order:
                    b = (base[0], base[1] + ahead)
                    if stage == "LOAD":
                        wait(sp, h2_stored, b, 16, -16)
                        gate(sp, "sp")
                        wait(sp, xn_ready[1], b, 2, -2)
                        gate(sp, "sp")
                        for t in range(TT):
                            src = mixed.rearrange("(c a) h l -> c h a l", a=NA)
                            src = src[bass.ds(b[0] * 2 + b[1], 1), t * P:(t + 1) * P, :, :].rearrange("c h a l -> (c h) a l")
                            sp.dma_start(h_sb[:, b[1] % 2, t, :].rearrange("q (a l) -> q a l", a=NA), src
                                         ).then_inc(h_in[b[1] % 2], 16)
                    if stage == "X2T" and n == 1:
                        wait(sp, h2_ready, b, 2, 2)
                        gate(sp, "sp")
                        sp.dma_start(h2_dram[bass.ds(b[0] * (2 * SEQ) + b[1] * SEQ, SEQ), :].rearrange("(t q) d -> q t d", q=P),
                                     h_sb[:, b[1] % 2]).then_inc(h2_stored, 16)
                        wait(sp, x2_ready, b, 2, 2)
                        gate(sp, "sp")
                        sp.dma_start(x2_dram[:, :, bass.ds(b[0] * (2 * SEQ) + b[1] * SEQ, SEQ)], x2_t[:]).then_inc(x2_stored, 16)

            walk(sp, stages)
            sp.wait_ge(h2_stored, 16 * BATCH)
            sp.wait_ge(x2_stored, 16 * BATCH)

        @block.gpsimd
        def _(pool):
            def normalise(j, b):
                wait(pool, newton[j], b, 5, 5)
                wait(pool, done["XT" if j == 0 else "X2T"], b, 2, 0)
                gate(pool, "pool")
                for t in range(TT):
                    pool.tensor_scalar(xn[j][:, t, :], h_sb[:, b[1] % 2, t, :], lnt[j][:, 4, t:t + 1],
                                       lnt[j][:, 5, t:t + 1], ALU.mult, ALU.add).then_inc(xn_ready[j], 1)

            def add_rope(part, b, t):
                wait(pool, rope_read, b, 4, 2 * part + t + 1)
                q = q_tok[:, b[1] % 2, t, 8 * part:8 * part + 8, 0:ROPE]
                pool.tensor_tensor(q, q, q_rot[:, t], ALU.add).then_inc(q_rope_ready, 1)

            def stages(order, base, first):
                for stage, ahead, n in order:
                    b = (base[0], base[1] + ahead)
                    if stage == "LNN":
                        normalise(0, b)
                    if stage == "LN2N":
                        normalise(1, b)
                    if stage == "QA":
                        add_rope(0, b, n)
                    if stage == "QB":
                        add_rope(1, b, n)
                    if stage == "REC":
                        wait(pool, recip_ready, b, HEADS, n + 1)
                        gate(pool, "pool")
                        for t, cols in enumerate((slice(0, P), slice(P, 3 * P))):
                            ins = pool.tensor_scalar(probs[:, n % RING, cols], probs[:, n % RING, cols],
                                                     recips[:, n, t:t + 1], 1.0, ALU.mult, ALU.mult)
                        ins.then_inc(norm_ready, 1)
                    if stage == "KRX":
                        wait(pool, kr_read, b, 1, 1)
                        pool.tensor_tensor(kr_s[:], kr_a[:], kr_b[:], ALU.add).then_inc(kr_sum, 1)
                        wait(pool, kr_sum, b, 1, 1)
                        wait(pool, done["S"], b, HEADS, 0)
                        gate(pool, "pool")
                        pool.tensor_scalar(k_t[0:ROPE, :, :], kr_s[:].unsqueeze(1).to_broadcast([ROPE, HEADS, SEQ]),
                                           1.0, 0.0, ALU.mult, ALU.add).then_inc(kr_ready, 1)

            walk(pool, stages)

        @block.scalar
        def _(act):
            act.preload_act_table_set("natural_log_exp_and_others")
            act.wait_ge(tables_in, 48)

            def guess(j, b):
                wait(act, var_ready[j], b, 1, 1)
                act.activation(lnt[j][:, 1, :], lnt[j][:, 0, :], ACT.Ln).then_inc(guess_ready[j], 1)
                wait(act, guess_ready[j], b, 2, 1)
                act.activation(lnt[j][:, 2, :], lnt[j][:, 1, :], ACT.Exp, scale=-0.5).then_inc(guess_ready[j], 1)

            def stages(order, base, first):
                use = 0
                for stage, ahead, n in order:
                    b = (base[0], base[1] + ahead)
                    half = b[1] % 2
                    ps = shared[use % 2]
                    use += stage in SHARED
                    if stage == "LNR":
                        guess(0, b)
                    if stage == "LN2R":
                        guess(1, b)
                    if stage == "XT":
                        wait(act, done["XT"], b, 2, n + 1)
                        wait(act, done["QB"], b, 2, 0)
                        act.activation(xt_hi[:, :, n * P:(n + 1) * P], ps[:].rearrange("q (k s) -> q k s", k=KD),
                                       ACT.Copy).then_inc(xt_hi_ready, 1)
                    if stage == "CKV":
                        wait(act, done["CKV"], b, 1, 1)
                        wait(act, done["V"], b, 2, 0)
                        wait(act, done["KN"], b, 2, 0)
                        act.activation(ck_hi[:], ps[:, 0:SEQ], ACT.Copy).then_inc(ck_hi_ready, 1)
                    if stage == "QN":
                        wait(act, done["QN"], b, 2, n + 1)
                        wait(act, done["QT"], b, 8, -8)
                        act.activation(q_tok[:, half, n, :, ROPE:DQK], ps[:].rearrange("q (h d) -> q h d", h=HEADS),
                                       ACT.Copy).then_inc(q_nope_ready, 1)
                    if stage == "KN":
                        wait(act, done["KN"], b, 2, n + 1)
                        wait(act, done["S"], b, HEADS, 0)
                        for j in range(2):
                            ins = act.activation(k_t[ROPE:DQK, 8 * n + j:8 * n + j + 5:4, :],
                                                 ps[32 * j:32 * j + 32, :].rearrange("q (g s) -> q g s", g=2), ACT.Copy)
                        ins.then_inc(kn_act, 1)
                    if stage == "V":
                        wait(act, done["V"], b, 2, n + 1)
                        wait(act, done["PV"], b, 4, -4)
                        act.activation(v_sb[:, half, n, :], ps[:], ACT.Copy).then_inc(v_ready, 1)
                    if stage == "X2T":
                        wait(act, done["X2T"], b, 2, n + 1)
                        wait(act, x2_stored, b, 16, 0)
                        act.activation(x2_t[:, :, n * P:(n + 1) * P], ps[:].rearrange("q (k s) -> q k s", k=KD),
                                       ACT.Copy).then_inc(x2_ready, 1)
                    if stage == "QT":
                        wait(act, done["QT"], b, 8, n + 1)
                        wait(act, done["S"], b, HEADS, 2 * n - 2 if n >= 2 else 0)
                        act.activation(q_t[:, n % 2], qt_bank[:], ACT.Copy).then_inc(qt_ready, 1)
                    if stage == "S":
                        wait(act, max_ready, b, HEADS, n + 1)
                        for t, cols in enumerate((slice(0, P), slice(P, 3 * P))):
                            ins = act.activation(probs[:, n % RING, cols], probs[:, n % RING, cols], ACT.Exp,
                                                 bias=neg_max[:, n, t:t + 1], scale=-1.0, accum_out=sums[:, n, t:t + 1])
                        ins.then_inc(exp_ready, 1)
                    if stage == "PT" and n in PT_ACT:
                        wait(act, done["PT"], b, HEADS, n + 1)
                        wait(act, done["PV"], b, 4, (n - RING) // 4 + 1 if n >= RING else 0)
                        act.activation(probs_t[:, n % RING, :], pt_bank[n % 2][:], ACT.Copy).then_inc(pt_act, 1)
                    if stage == "PV":
                        wait(act, done["PV"], b, 4, n + 1)
                        wait(act, done["WO"], b, 2, 0)
                        act.activation(o_hi[:, n, :], pv_bank[:], ACT.Copy).then_inc(o_hi_ready, 1)

            walk(act, stages)

        @block.vector
        def _(dve):
            dve.wait_ge(tables_in, 48)

            def statistics(j, b):
                h = h_sb[:, b[1] % 2]
                wait(dve, xn_ready[j], b, 2, 0)
                if j == 0:
                    dve.wait_ge(h_in[b[1] % 2], b[0] * 32 + (b[1] // 2 * 32 + 32))
                else:
                    wait(dve, h2_ready, b, 2, 2)
                for t in range(TT):
                    dve.bn_stats(stats[j][:, t, :], h[:, t, :]).then_inc(stat_done[j], 1)
                wait(dve, stat_done[j], b, 4, 2)
                gate(dve, "dve")
                for t in range(TT):
                    dve.bn_aggr(meanvar[j][:, t, :], stats[j][:, t, :]).then_inc(stat_done[j], 1)
                wait(dve, stat_done[j], b, 4, 4)
                dve.tensor_scalar(lnt[j][:, 0, :], meanvar[j][:, :, 1], EPS, None, ALU.add).then_inc(var_ready[j], 1)

            def newton_step(j, b):
                v, g, s, y, m = (lnt[j][:, k, :] for k in (0, 2, 3, 4, 5))
                wait(dve, guess_ready[j], b, 2, 2)
                dve.tensor_tensor(s, g, g, ALU.mult).then_inc(newton[j], 1)
                wait(dve, newton[j], b, 5, 1)
                dve.tensor_tensor(s, s, v, ALU.mult).then_inc(newton[j], 1)
                wait(dve, newton[j], b, 5, 2)
                dve.tensor_scalar(s, s, -0.5, 1.5, ALU.mult, ALU.add).then_inc(newton[j], 1)
                wait(dve, newton[j], b, 5, 3)
                dve.tensor_tensor(y, g, s, ALU.mult).then_inc(newton[j], 1)
                wait(dve, newton[j], b, 5, 4)
                dve.scalar_tensor_tensor(out=m, in0=meanvar[j][:, :, 0], scalar=-1.0, in1=y,
                                         op0=ALU.mult, op1=ALU.mult).then_inc(newton[j], 1)

            def rotate(part, b, t, ps):
                x = ps[:].rearrange("q (h d) -> q h d", h=8)
                r = 2 * part + t
                wait(dve, done["QA" if part == 0 else "QB"], b, 2, t + 1)
                if part == 0:
                    wait(dve, done["QT"], b, 8, -8)
                wait(dve, q_rope_ready, b, 4, r - 1 if r >= 2 else 0)
                dve.tensor_tensor(q_tok[:, b[1] % 2, t, 8 * part:8 * part + 8, 0:ROPE], x,
                                  cos_sin[:, 0, t, :].unsqueeze(1).to_broadcast([P, 8, ROPE]), ALU.mult)
                dve.tensor_tensor(q_rot[:, t].rearrange("q h (a d) -> q h a d", a=2),
                                  x.rearrange("q h (a d) -> q h a d", a=2)[:, :, ::-1, :],
                                  cos_sin[:, 1, t, :].rearrange("q (a d) -> q a d", a=2).unsqueeze(1).to_broadcast([P, 8, 2, ROPE // 2]),
                                  ALU.mult).then_inc(rope_read, 1)

            def stages(order, base, first):
                use = 0
                for stage, ahead, n in order:
                    b = (base[0], base[1] + ahead)
                    ps = shared[use % 2]
                    use += stage in SHARED
                    if stage == "LNS":
                        statistics(0, b)
                    if stage == "LN2S":
                        statistics(1, b)
                    if stage == "LNN":
                        newton_step(0, b)
                    if stage == "LN2N":
                        newton_step(1, b)
                    if stage == "XT":
                        wait(dve, xt_hi_ready, b, 2, n + 1)
                        dve.tensor_tensor(xt_lo[:, :, n * P:(n + 1) * P], ps[:].rearrange("q (k s) -> q k s", k=KD),
                                          xt_hi[:, :, n * P:(n + 1) * P].bitcast(F32), ALU.subtract).then_inc(xt_lo_ready, 1)
                    if stage == "CKV":
                        wait(dve, ck_hi_ready, b, 1, 1)
                        dve.tensor_tensor(ck_lo[:], ps[:, 0:SEQ], ck_hi[:].bitcast(F32), ALU.subtract).then_inc(ck_lo_ready, 1)
                    if stage == "KR":
                        wait(dve, done["KR"], b, 1, 1)
                        wait(dve, kr_sum, b, 1, 0)
                        dve.tensor_tensor(kr_a[:], ps[0:ROPE, 0:SEQ], cos_sin_t[0:ROPE, :], ALU.mult)
                        dve.tensor_tensor(kr_b[:], ps[ROPE:P, 0:SEQ], cos_sin_t[ROPE:P, :], ALU.mult).then_inc(kr_read, 1)
                    if stage == "QA":
                        rotate(0, b, n, ps)
                    if stage == "QB":
                        rotate(1, b, n, ps)
                    if stage == "KN":
                        wait(dve, done["KN"], b, 2, n + 1)
                        wait(dve, done["S"], b, HEADS, 0)
                        for j in range(2, 4):
                            ins = dve.tensor_copy(k_t[ROPE:DQK, 8 * n + j:8 * n + j + 5:4, :],
                                                  ps[32 * j:32 * j + 32, :].rearrange("q (g s) -> q g s", g=2))
                        ins.then_inc(kn_dve, 1)
                    if stage == "WO":
                        wait(dve, done["WO"], b, 2, n + 1)
                        h = h_sb[:, b[1] % 2, n, :]
                        dve.tensor_tensor(h, ps[:], h, ALU.add).then_inc(h2_ready, 1)
                    if stage == "S":
                        wait(dve, done["S"], b, HEADS, n + 1)
                        wait(dve, done["PT"], b, HEADS, n - RING + 1 if n >= RING else 0)
                        gate(dve, "dve")
                        for t, cols in enumerate((slice(0, P), slice(P, 3 * P))):
                            ins = dve.tensor_tensor_reduce(probs[:, n % RING, cols], s_bank[n % 2][:, cols], mask[:, cols],
                                                           -SCALE, 3.0e38, ALU.add, ALU.min, neg_max[:, n, t:t + 1])
                        ins.then_inc(max_ready, 1)
                    if stage == "REC":
                        wait(dve, exp_ready, b, HEADS, n + 1)
                        dve.reciprocal(recips[:, n, :], sums[:, n, :]).then_inc(recip_ready, 1)
                    if stage == "PT" and n not in PT_ACT:
                        wait(dve, done["PT"], b, HEADS, n + 1)
                        wait(dve, done["PV"], b, 4, (n - RING) // 4 + 1 if n >= RING else 0)
                        dve.tensor_copy(probs_t[:, n % RING, :], pt_bank[n % 2][:]).then_inc(pt_dve, 1)
                    if stage == "PV":
                        wait(dve, o_hi_ready, b, 4, n + 1)
                        dve.tensor_tensor(o_lo[:, n, :], pv_bank[:], o_hi[:, n, :].bitcast(F32),
                                          ALU.subtract).then_inc(o_lo_ready, 1)

            walk(dve, stages)

        @block.tensor
        def _(pe):
            pe.wait_ge(tables_in, 48)

            def three(out, pairs, width=None):
                for n, ((lh, ll), (rh, rl)) in enumerate(pairs):
                    pe.matmul(out, lh, rh, start=n == 0, stop=False)
                    pe.matmul(out, lh, rl, start=False, stop=False)
                    last = pe.matmul(out, ll, rh, start=False, stop=n == len(pairs) - 1)
                return last

            def weight(col, width):
                return whi[:, col:col + width], wlo[:, col:col + width]

            def x_of(k, cols):
                return xt_hi[:, k, cols], xt_lo[:, k, cols]

            def pt_copied(b, h):
                copies = sum(x <= h for x in PT_ACT)
                wait(pe, pt_act, b, len(PT_ACT), copies)
                wait(pe, pt_dve, b, HEADS - len(PT_ACT), h + 1 - copies)

            def stages(order, base, first):
                uses = [s for s in order if s[0] in SHARED]
                use = 0
                for stage, ahead, n in order:
                    b = (base[0], base[1] + ahead)
                    half = b[1] % 2
                    tile = slice(n * P, (n + 1) * P)
                    if stage in SHARED:
                        ps = shared[use % 2]
                        if use >= 2:
                            was, ahead_was, n_was = uses[use - 2]
                            b_was = (base[0], base[1] + ahead_was)
                            for s, per in FREES[was]:
                                wait(pe, s, b_was, per, n_was + 1 + (2 if was == "QB" else 0))
                        elif not first:
                            wait(pe, x2_ready, base, 2, 0)
                            wait(pe, kn_act, base, 2, 2)
                            wait(pe, kn_dve, base, 2, 2)
                        use += 1
                    if stage in ("XT", "X2T"):
                        j = 0 if stage == "XT" else 1
                        wait(pe, xn_ready[j], b, 2, n + 1)
                        for k in range(KD):
                            last = pe.transpose(ps[:, k * P:(k + 1) * P], xn[j][:, n, k * P:(k + 1) * P], ident[:])
                    if stage == "CKV":
                        wait(pe, xt_lo_ready, b, 2, 2)
                        last = three(ps[:, 0:SEQ], [(weight(WDKV + k * LATENT, LATENT), x_of(k, slice(0, SEQ))) for k in range(KD)])
                    if stage == "KR":
                        last = three(ps[:, 0:SEQ], [(weight(WKR + k * 2 * ROPE, 2 * ROPE), x_of(k, slice(0, SEQ))) for k in range(KD)])
                    if stage in ("QN", "QA", "QB"):
                        col = WQ + ("QN", "QA", "QB").index(stage) * 512
                        last = three(ps[:], [(x_of(k, tile), weight(col + k * HEADS * DQK, 512)) for k in range(KD)])
                    if stage == "KN":
                        wait(pe, ck_lo_ready, b, 1, 1)
                        for g in range(2):
                            last = three(ps[:, g * SEQ:(g + 1) * SEQ],
                                         [(weight(WUK + (2 * n + g) * P, P), (ck_hi[:], ck_lo[:]))])
                    if stage == "V":
                        wait(pe, ck_lo_ready, b, 1, 1)
                        last = three(ps[:], [((ck_hi[:, tile], ck_lo[:, tile]), weight(WUV, 512))])
                    if stage == "WO":
                        wait(pe, o_lo_ready, b, 4, 4)
                        last = three(ps[:], [((o_hi[:, g, tile], o_lo[:, g, tile]), weight(WO + g * DIM, DIM)) for g in range(KD)])
                    if stage == "QT":
                        if n == 0:
                            wait(pe, q_nope_ready, b, 2, 2)
                        if n in (0, 4):
                            wait(pe, q_rope_ready, b, 4, 2 if n == 0 else 4)
                        wait(pe, qt_ready, b, 8, n)
                        for h in range(2):
                            for t in range(TT):
                                last = pe.transpose(qt_bank[:, h, t * P:(t + 1) * P], q_tok[:, half, t, 2 * n + h, :], ident[:])
                    if stage == "S":
                        if n == 0:
                            wait(pe, kn_act, b, 2, 2)
                            wait(pe, kn_dve, b, 2, 2)
                            wait(pe, kr_ready, b, 1, 1)
                        wait(pe, qt_ready, b, 8, n // 2 + 1)
                        wait(pe, max_ready, b, HEADS, n - 1 if n >= 2 else 0)
                        q = q_t[:, n // 2 % 2, n % 2, :]
                        pe.matmul(s_bank[n % 2][:, 0:P], q[:, 0:P], k_t[:, n, 0:P], start=True, stop=True)
                        last = pe.matmul(s_bank[n % 2][:, P:3 * P], q[:, P:SEQ], k_t[:, n, :], start=True, stop=True)
                    if stage == "PT":
                        wait(pe, norm_ready, b, HEADS, n + 1)
                        if n >= 2:
                            pt_copied(b, n - 2)
                        else:
                            pt_copied(b, -1)
                        for k in range(3):
                            last = pe.transpose(pt_bank[n % 2][:, k * P:(k + 1) * P], probs[:, n % RING, k * P:(k + 1) * P], ident[:])
                    if stage == "PV":
                        pt_copied(b, 4 * n + 3)
                        wait(pe, v_ready, b, 2, 2)
                        wait(pe, o_lo_ready, b, 4, n)
                        for k, (src, dst) in enumerate(((slice(0, SEQ), slice(0, SEQ)), (slice(SEQ, SEQ + P), slice(P, SEQ)))):
                            for j in range(4):
                                h = 4 * n + j
                                last = pe.matmul(pv_bank[32 * j:32 * j + 32, dst], v_sb[:, half, k, h * DH:(h + 1) * DH],
                                                 probs_t[:, h % RING, src], start=k == 0, stop=k == 1, tile_position=(0, 32 * j))
                    if stage in done:
                        last.then_inc(done[stage], 1)

            walk(pe, stages)


def feed_forward(nc, x2_dram, h2_dram, w_up, w_down, bias_up, bias_down, out):
    with ExitStack() as ctx:
        def sb(name, shape, dt=F32):
            return ctx.enter_context(nc.sbuf_tensor(name, shape, dt))

        def bank(name, shape):
            return ctx.enter_context(nc.psum_tensor(name, shape, F32))

        def sem(name):
            return ctx.enter_context(nc.semaphore(name))

        CH = 512
        NC = TOKENS // CH
        NT = CH // P
        NM = HIDDEN // P
        RAW = 3
        G = 3
        up_hi = sb("up_hi", [P, NM, KD, P], F32R)
        up_lo = sb("up_lo", [P, NM, KD, P], F32R)
        down_hi = sb("down_hi", [P, NM, DIM], F32R)
        down_lo = sb("down_lo", [P, NM, DIM], F32R)
        raw = sb("raw", [P, RAW, 2, DIM])
        b1 = sb("b1", [P, NM])
        b2 = sb("b2", [P, DIM])
        x_raw = sb("x_raw", [P, KD, CH])
        x_hi = sb("x_hi", [P, KD, CH], F32R)
        x_lo = sb("x_lo", [P, KD, CH], F32R)
        g_raw = sb("g_raw", [P, 2, CH])
        g_hi = sb("g_hi", [P, G, CH], F32R)
        g_lo = sb("g_lo", [P, G, CH], F32R)
        res = sb("res", [P, NT, DIM])
        up_bank = [bank(f"up_bank{i}", [P, CH]) for i in range(2)]
        out_bank = [bank(f"out_bank{i}", [P, DIM]) for i in range(NT)]

        raw_in = [sem(f"raw_in{i}") for i in range(RAW)]
        bias_in, x_in, res_in, w_ready, w_half = map(sem, ("bias_in", "x_in", "res_in", "w_ready", "w_half"))
        x_hi_ready, x_lo_ready, up_done, gelu_done, g_hi_ready, g_lo_ready = map(
            sem, ("x_hi_ready", "x_lo_ready", "up_done", "gelu_done", "g_hi_ready", "g_lo_ready"))
        down_done, res_biased, out_ready, out_stored, gate_sp = map(
            sem, ("down_done", "res_biased", "out_ready", "out_stored", "gate_sp"))
        block = ctx.enter_context(nc.Block())

        @block.sync
        def _(sp):
            def load_x(c):
                sp.wait_ge(x_lo_ready, c * KD)
                sp.sem_inc(gate_sp, 1)
                sp.dma_start(x_raw[:], x2_dram[:, :, bass.ds(c * CH, CH)]).then_inc(x_in, 16)

            def load_res(c):
                sp.wait_ge(out_stored, c * (16 * NT))
                sp.sem_inc(gate_sp, 1)
                sp.dma_start(res[:], h2_dram[bass.ds(c * CH, CH), :].rearrange("(t q) d -> q t d", q=P)).then_inc(res_in, 16)

            def store(c):
                for t in range(NT):
                    sp.wait_ge(out_ready, c * NT + (t + 1))
                    sp.sem_inc(gate_sp, 1)
                    sp.dma_start(out[bass.ds(c * CH + t * P, P), :], res[:, t, :]).then_inc(out_stored, 16)

            sp.dma_start(x_raw[:], x2_dram[:, :, 0:CH]).then_inc(x_in, 16)
            sp.dma_start(b1[:], bias_up).then_inc(bias_in, 16)
            sp.dma_start(b2[:], bias_down.rearrange("(a d) -> a d", a=1).to_broadcast([P, DIM])).then_inc(bias_in, 16)
            for m in range(NM):
                if m >= RAW:
                    sp.wait_ge(w_ready, 2 * (m - RAW) + 2)
                sp.dma_start(raw[:, m % RAW, 0, :], w_up[:, m, :]).then_inc(raw_in[m % RAW], 16)
                sp.dma_start(raw[:, m % RAW, 1, :], w_down[:, m, :]).then_inc(raw_in[m % RAW], 16)
            with sp.Fori(0, NC - 1) as c:
                load_res(c)
                load_x(c + 1)
                store(c)
            load_res(NC - 1)
            store(NC - 1)
            sp.wait_ge(out_stored, 16 * NT * NC)

        @block.gpsimd
        def _(pool):
            def split_x(c):
                for k in range(KD):
                    pool.wait_ge(x_hi_ready, c * KD + (k + 1))
                    pool.tensor_tensor(x_lo[:, k, :], x_raw[:, k, :], x_hi[:, k, :].bitcast(F32),
                                       ALU.subtract).then_inc(x_lo_ready, 1)

            def add_bias(c):
                pool.wait_ge(res_in, c * 16 + 16)
                for t in range(NT):
                    pool.tensor_tensor(res[:, t, :], res[:, t, :], b2[:], ALU.add).then_inc(res_biased, 1)

            split_x(0)
            pool.wait_ge(bias_in, 32)
            for m in range(NM):
                pool.wait_ge(raw_in[m % RAW], 32 * (m // RAW + 1))
                for part, (hi, lo) in enumerate(((up_hi[:, m].rearrange("q k j -> q (k j)"), up_lo[:, m].rearrange("q k j -> q (k j)")),
                                                 (down_hi[:, m, :], down_lo[:, m, :]))):
                    pool.tensor_scalar(hi, raw[:, m % RAW, part, :], 1.0, 1.0, ALU.mult, ALU.mult).then_inc(w_half, 1)
                    pool.wait_ge(w_half, 2 * m + part + 1)
                    pool.tensor_tensor(lo, raw[:, m % RAW, part, :], hi.bitcast(F32), ALU.subtract).then_inc(w_ready, 1)
            add_bias(0)
            with pool.Fori(1, NC) as c:
                split_x(c)
                add_bias(c)

        @block.scalar
        def _(act):
            act.wait_ge(bias_in, 32)
            with act.Fori(0, NC) as c:
                act.wait_ge(x_in, c * 16 + 16)
                act.wait_ge(up_done, c * NM)
                for k in range(KD):
                    act.activation(x_hi[:, k, :], x_raw[:, k, :], ACT.Copy).then_inc(x_hi_ready, 1)
                for m in range(NM):
                    act.wait_ge(up_done, c * NM + (m + 1))
                    act.wait_ge(g_lo_ready, c * NM + (m - 1 if m >= 2 else 0))
                    act.activation(g_raw[:, m % 2, :], up_bank[m % 2][:], ACT.Gelu, bias=b1[:, m:m + 1]).then_inc(gelu_done, 1)
                    act.wait_ge(gelu_done, c * NM + (m + 1))
                    act.wait_ge(down_done, c * NM + (m - G + 1 if m >= G else 0))
                    act.activation(g_hi[:, m % G, :], g_raw[:, m % 2, :], ACT.Copy).then_inc(g_hi_ready, 1)

        @block.vector
        def _(dve):
            with dve.Fori(0, NC) as c:
                for m in range(NM):
                    dve.wait_ge(g_hi_ready, c * NM + (m + 1))
                    dve.tensor_tensor(g_lo[:, m % G, :], g_raw[:, m % 2, :], g_hi[:, m % G, :].bitcast(F32),
                                      ALU.subtract).then_inc(g_lo_ready, 1)
                dve.wait_ge(down_done, c * NM + NM)
                for t in range(NT):
                    dve.wait_ge(res_biased, c * NT + (t + 1))
                    dve.tensor_tensor(res[:, t, :], out_bank[t][:], res[:, t, :], ALU.add).then_inc(out_ready, 1)

        @block.tensor
        def _(pe):
            def up(c, m):
                if m < 2:
                    pe.wait_ge(gelu_done, c * NM)
                else:
                    pe.wait_ge(gelu_done, c * NM + (m - 1))
                pe.wait_ge(w_ready, 2 * m + 2)
                for k in range(KD):
                    if m == 0:
                        pe.wait_ge(x_lo_ready, c * KD + (k + 1))
                    pe.matmul(up_bank[m % 2][:], up_hi[:, m, k, :], x_hi[:, k, :], start=k == 0, stop=False)
                    pe.matmul(up_bank[m % 2][:], up_hi[:, m, k, :], x_lo[:, k, :], start=False, stop=False)
                    last = pe.matmul(up_bank[m % 2][:], up_lo[:, m, k, :], x_hi[:, k, :], start=False, stop=k == KD - 1)
                last.then_inc(up_done, 1)

            def down(c, m):
                pe.wait_ge(g_lo_ready, c * NM + (m + 1))
                if m == 0:
                    pe.wait_ge(out_ready, c * NT)
                for t in range(NT):
                    rows = slice(t * P, (t + 1) * P)
                    pe.matmul(out_bank[t][:], g_hi[:, m % G, rows], down_hi[:, m, :], start=m == 0, stop=False)
                    pe.matmul(out_bank[t][:], g_hi[:, m % G, rows], down_lo[:, m, :], start=False, stop=False)
                    last = pe.matmul(out_bank[t][:], g_lo[:, m % G, rows], down_hi[:, m, :], start=False, stop=m == NM - 1)
                last.then_inc(down_done, 1)

            with pe.Fori(0, NC) as c:
                for m in range(NM):
                    up(c, m)
                    if m >= 2:
                        down(c, m - 2)
                down(c, NM - 2)
                down(c, NM - 1)


def vit_layer(nc, c_parts, log_dt, log_w_real, w_imag, weights, rope_tok, rope_feat, causal,
              w_up, w_down, bias_up, bias_down, out):
    assert SEQ == TT * P and DIM == KD * P and HEADS * DH == DIM and NA * NI * NJ == DIM
    mixed = nc.dram_tensor("mixed", [P, SEQ, NI * NJ], F32).ap()
    h2_dram = nc.dram_tensor("h2_dram", [TOKENS, DIM], F32).ap()
    x2_dram = nc.dram_tensor("x2_dram", [P, KD, TOKENS], F32).ap()
    with ExitStack() as ctx:
        whi = ctx.enter_context(nc.sbuf_tensor("whi", [P, WCOLS], F32R))
        wlo = ctx.enter_context(nc.sbuf_tensor("wlo", [P, WCOLS], F32R))
        ident = ctx.enter_context(nc.sbuf_tensor("ident", [P, P], F32))
        token_mixer(nc, c_parts, log_dt, log_w_real, w_imag, weights, whi, wlo, ident, mixed)
        attention(nc, mixed, whi, wlo, ident, rope_tok, rope_feat, causal, h2_dram, x2_dram)
    feed_forward(nc, x2_dram, h2_dram, w_up, w_down, bias_up, bias_down, out)


def kernel(x, L0_tok_log_dt, L0_tok_log_w_real, L0_tok_w_imag, L0_attn_Wq, L0_attn_Wdkv, L0_attn_Wkr, L0_attn_Wukv,
           L0_attn_Wo, L0_ffn_proj1, L0_ffn_proj1_bias, L0_ffn_proj2, L0_ffn_proj2_bias, L0_ffn_gate_w):
    import numpy as np
    import concourse.bacc as bacc
    from concourse.bass_utils import run_bass_kernel_spmd

    def tiles(w):
        k, n = w.shape
        return w.reshape(k // P, P, n).transpose(1, 0, 2).reshape(P, -1)

    wq = np.asarray(L0_attn_Wq).reshape(DIM, HEADS, DQK)
    wq = np.concatenate([wq[:, :, :DH].reshape(DIM, -1), wq[:, :, DH:].reshape(DIM, -1)], axis=1)
    wkr = np.asarray(L0_attn_Wkr)
    wkr = np.concatenate([wkr, wkr[:, ROPE // 2:], wkr[:, :ROPE // 2]], axis=1)
    wukv = np.asarray(L0_attn_Wukv).reshape(LATENT, HEADS, 2 * DH)
    weights = np.concatenate([tiles(wq), tiles(np.asarray(L0_attn_Wdkv)), tiles(wkr),
                              wukv[:, :, :DH].reshape(LATENT, -1), wukv[:, :, DH:].reshape(LATENT, -1),
                              tiles(np.asarray(L0_attn_Wo))], axis=1)

    inv_freq = (1.0 / 10000.0 ** (np.arange(0, ROPE, 2, dtype=np.float32) / ROPE)).astype(np.float32)
    angle = np.arange(SEQ, dtype=np.float32)[:, None] * inv_freq[None, :]
    cos = np.cos(np.concatenate([angle, angle], 1)).astype(np.float32)
    sin = np.sin(np.concatenate([-angle, angle], 1)).astype(np.float32)
    rope_tok = np.stack([cos, sin]).reshape(2, TT, P, ROPE).transpose(2, 0, 1, 3)
    rope_feat = np.concatenate([cos.T, sin.T], axis=0)
    diagonal = np.where(np.tril(np.ones((P, P), bool)), 0.0, MASKED).astype(np.float32)
    causal = np.concatenate([diagonal, np.zeros((P, P), np.float32), diagonal], axis=1)

    arrays = {
        "c_parts": np.asarray(x).transpose(3, 2, 1, 0),
        "log_dt": np.asarray(L0_tok_log_dt),
        "log_w_real": np.asarray(L0_tok_log_w_real).T,
        "w_imag": np.asarray(L0_tok_w_imag).T,
        "weights": weights,
        "rope_tok": rope_tok,
        "rope_feat": rope_feat,
        "causal": causal,
        "w_up": np.asarray(L0_ffn_proj1).reshape(HIDDEN // P, P, KD, P).transpose(3, 0, 2, 1).reshape(P, HIDDEN // P, DIM),
        "w_down": np.asarray(L0_ffn_proj2).reshape(DIM, HIDDEN // P, P).transpose(2, 1, 0),
        "bias_up": np.asarray(L0_ffn_proj1_bias).reshape(HIDDEN // P, P).T,
        "bias_down": np.asarray(L0_ffn_proj2_bias),
    }
    arrays = {k: np.ascontiguousarray(v) for k, v in arrays.items()}
    nc = bacc.Bacc("TRN2", target_bir_lowering=False, num_devices=1)
    args = [nc.dram_tensor(k, v.shape, mybir.dt.from_np(v.dtype), kind="ExternalInput").ap() for k, v in arrays.items()]
    out = nc.dram_tensor("out", (TOKENS, DIM), F32, kind="ExternalOutput").ap()
    vit_layer(nc, *args, out)
    r = run_bass_kernel_spmd(nc, [arrays], core_ids=[0])
    return r.results[0]["out"].reshape(BATCH, SEQ, DIM)
```

```python
from contextlib import ExitStack

import concourse.bass as bass
from concourse import mybir

F32 = mybir.dt.float32
F32R = mybir.dt.float32r
I32 = mybir.dt.int32
ALU = mybir.AluOpType
ACT = mybir.ActivationFunctionType

P = 128
BATCH, SEQ, DIM = 16, 256, 512
MODES = 64
TOKENS = BATCH * SEQ
HEADS, DH, ROPE, LATENT = 16, 32, 64, 128
DQK = DH + ROPE
HIDDEN = 2048
KD = DIM // P
TT = SEQ // P
EPS = 1e-5
SCALE = 1.0 / (DQK ** 0.5)
MASKED = -1e10

WQ, WDKV, WKR = 0, KD * HEADS * DQK, KD * (HEADS * DQK + LATENT)
WUK = WKR + KD * 2 * ROPE
WUV = WUK + HEADS * DH
WO = WUV + HEADS * DH
WCOLS = WO + KD * DIM
WCHUNK = 1024

NA, NI, NJ = 8, 8, 8
HC = 128
HB = 8

MAGIC = 1.5 * 2.0 ** 23
LOG2E, LN2_HI, LN2_LO = 1.4426950408889634, 0.693359375, -2.12194440054690583e-4
PI = 3.141592653589793
C1 = 6.283203125
C2 = 2 * PI - C1
PI_BELOW = 3.1415925


def dve_chain(dve, sem):
    count = [0]

    def link(ins):
        count[0] += 1
        ins.then_inc(sem, 1)
        dve.wait_ge(sem, count[0])

    return link


def token_mixer(nc, c_parts, log_dt, log_w_real, w_imag, weights, whi, wlo, ident, mixed):
    with ExitStack() as ctx:
        def sb(name, shape, dt=F32):
            return ctx.enter_context(nc.sbuf_tensor(name, shape, dt))

        def sem(name):
            return ctx.enter_context(nc.semaphore(name))

        logs = sb("logs", [P, 2, SEQ])
        wim = sb("wim", [P, SEQ])
        dtw = sb("dtw", [P, 2, SEQ])
        dre = sb("dre", [P, SEQ])
        dim = sb("dim", [P, SEQ])
        half_pi = sb("half_pi", [P, 1])
        cbuf = sb("cbuf", [P, 2, HC, BATCH])
        pim = sb("pim", [P, NI, HC])
        vj_a = sb("vj_a", [P, NJ, HC])
        vj_b = sb("vj_b", [P, NJ, HC])
        za_b_pool = sb("za_b_pool", [P, NA, HC])
        ang = sb("ang", [P, 2, 8, HC])
        kbuf = sb("kbuf", [P, 2, 8, HC])
        re_t = sb("re_t", [P, 8, HC])
        im_t = sb("im_t", [P, 2, 8, HC])
        mag = sb("mag", [P, 3, 8, HC])
        step_sc = sb("step_sc", [P, 3, HC])
        gt = sb("gt", [P, 6, HC])
        g_re = sb("g_re", [P, 1, HC])
        g_im = sb("g_im", [P, 1, HC])
        inv2 = sb("inv2", [P, SEQ])
        w_sq = sb("w_sq", [P, SEQ])
        v_t1 = sb("v_t1", [P, 2, HB, NI * NJ])
        v_t2 = sb("v_t2", [P, 2, HB, NI * NJ])
        vblk = sb("vblk", [P, 2, HB, NI * NJ])
        w1 = sb("w1", [P, 2, HB, BATCH * NA])
        w2 = sb("w2", [P, 2, HB, BATCH * NA])
        ystage = sb("ystage", [P, 2, HB * NI * NJ])
        wraw = sb("wraw", [P, 2, WCHUNK])
        pre = ctx.enter_context(nc.psum_tensor("pre", [P, NI, HC], F32))
        za_a = ctx.enter_context(nc.psum_tensor("za_a", [P, NA, HC], F32))
        za_b = ctx.enter_context(nc.psum_tensor("za_b", [P, NA, HC], F32))
        ypsum = [ctx.enter_context(nc.psum_tensor(f"ypsum{i}", [P, HB * NI * NJ], F32)) for i in range(2)]

        params_in, c_in, chain, consts_ready, ident_ready = map(
            sem, ("params_in", "c_in", "chain", "consts_ready", "ident_ready"))
        wraw_in = [sem(f"wraw_in{i}") for i in range(2)]
        whi_ready, wlo_ready = sem("whi_ready"), sem("wlo_ready")
        steps_ready, exps_ready, angle_ready, abs_ready, sin_ready, cos_ready, half_ready = map(
            sem, ("steps_ready", "exps_ready", "angle_ready", "abs_ready", "sin_ready", "cos_ready", "half_ready"))
        scaled, za_b_copied, inv2_ready, g_chain, g_ready, tables_ready, c_used = map(
            sem, ("scaled", "za_b_copied", "inv2_ready", "g_chain", "g_ready", "tables_ready", "c_used"))
        vt1_ready, vt2_ready, v_ready, w1_ready, w2_pool, w2_dve, w_sum = map(
            sem, ("vt1_ready", "vt2_ready", "v_ready", "w1_ready", "w2_pool", "w2_dve", "w_sum"))
        block_done, y_out, gate_sp = map(sem, ("block_done", "y_out", "gate_sp"))
        y_stored = [sem(f"y_stored{i}") for i in range(2)]

        NCH = SEQ // HC
        NB = HC // HB
        NW = WCOLS // WCHUNK
        FIRST_SPLIT = 4
        GROUPS = ("j", "p", "a")
        EXPS = {"j": list(range(NJ)), "p": [NJ * i for i in range(NI)], "a": [NI * NJ * a for a in range(NA)]}
        lo, up = slice(0, MODES), slice(MODES, P)
        block = ctx.enter_context(nc.Block())

        @block.sync
        def _(sp):
            sp.dma_start(logs[:, 0, :], log_dt.rearrange("(a h) -> a h", a=1).to_broadcast([P, SEQ])).then_inc(params_in, 16)
            for half in range(2):
                rows = slice(half * MODES, (half + 1) * MODES)
                sp.dma_start(logs[rows, 1, :], log_w_real).then_inc(params_in, 16)
                sp.dma_start(wim[rows, :], w_imag).then_inc(params_in, 16)
            for chunk in range(NCH):
                if chunk:
                    sp.wait_ge(c_used, chunk)
                for half in range(2):
                    sp.dma_start(cbuf[half * MODES:(half + 1) * MODES, :, :, :],
                                 c_parts[:, :, chunk * HC:(chunk + 1) * HC, :].rearrange("r n h c -> n r h c")
                                 ).then_inc(c_in, 16)
                with sp.Fori(0, NB // 2) as i:
                    for p in range(2):
                        n = i * 2 + (chunk * NB + p)
                        sp.wait_ge(y_out, n + 2)
                        sp.sem_inc(gate_sp, 1)
                        sp.dma_start(mixed[:, bass.ds(i * (2 * HB) + (chunk * HC + p * HB), HB), :],
                                     ystage[:, p, :].rearrange("q (h l) -> q h l", h=HB)).then_inc(y_stored[p], 16)
            for p in range(2):
                sp.wait_ge(y_stored[p], 8 * NCH * NB)

        @block.gpsimd
        def _(pool):
            pool.memset(half_pi[:], PI / 2).then_inc(consts_ready, 1)
            pool.memset(ident[:], 0.0).then_inc(ident_ready, 1)
            pool.wait_ge(ident_ready, 1)
            pool.affine_select(out=ident[:], in_=ident[:], compare_op=ALU.not_equal, fill=1.0, base=0,
                               pattern=[[-1, P]], channel_multiplier=1).then_inc(ident_ready, 1)

            links = [0]

            def link(ins):
                links[0] += 1
                ins.then_inc(g_chain, 1)
                pool.wait_ge(g_chain, links[0])

            def low_parts(chunks):
                for n in chunks:
                    cols = slice(n * WCHUNK, (n + 1) * WCHUNK)
                    pool.wait_ge(whi_ready, n + 1)
                    pool.tensor_tensor(wlo[:, cols], wraw[:, n % 2, :], whi[:, cols].bitcast(F32),
                                       ALU.subtract).then_inc(wlo_ready, 1)

            def at(chunk):
                return FIRST_SPLIT + chunk * len(GROUPS)

            low_parts(range(FIRST_SPLIT))
            for chunk in range(NCH):
                hs = slice(chunk * HC, (chunk + 1) * HC)
                g = [gt[:, k, :] for k in range(6)]
                wr, wi = dtw[:, 1, hs], wim[:, hs]
                pool.wait_ge(inv2_ready, 1)
                pool.wait_ge(half_ready, chunk + 1)
                if chunk:
                    pool.wait_ge(tables_ready, chunk)
                ex, ni = mag[:, 0, 1, :], g[1]
                pool.tensor_tensor(ni, ex, step_sc[:, 1, :], ALU.mult)
                pool.tensor_scalar(g[0], ex, 1.0, 1.0, ALU.mult, ALU.add)
                link(pool.tensor_tensor(g[2], step_sc[:, 2, :], step_sc[:, 2, :], ALU.mult))
                pool.tensor_scalar(g[3], g[2], -2.0, 1.0, ALU.mult, ALU.add)
                pool.tensor_scalar(g[2], g[2], -2.0, 1.0, ALU.mult, ALU.mult)
                link(pool.tensor_tensor(g[0], g[0], step_sc[:, 0, :], ALU.mult))
                link(pool.tensor_tensor(g[0], g[0], g[3], ALU.mult))
                link(pool.tensor_tensor(g[0], g[0], g[2], ALU.add))
                pool.tensor_tensor(g[2], ni, wi, ALU.mult)
                pool.tensor_tensor(g[3], g[0], wr, ALU.mult)
                pool.tensor_tensor(g[4], ni, wr, ALU.mult)
                link(pool.tensor_tensor(g[5], g[0], wi, ALU.mult))
                pool.tensor_tensor(g[2], g[2], g[3], ALU.subtract)
                link(pool.tensor_tensor(g[4], g[4], g[5], ALU.add))
                link(pool.tensor_scalar(g[4], g[4], -1.0, 1.0, ALU.mult, ALU.mult))
                pool.tensor_tensor(g_re[:, 0, :], g[2], inv2[:, hs], ALU.mult)
                pool.tensor_tensor(g_im[:, 0, :], g[4], inv2[:, hs], ALU.mult).then_inc(g_ready, 1)

                low_parts(range(at(chunk), NW if chunk == NCH - 1 else at(chunk + 1)))
                pool.wait_ge(tables_ready, chunk + 1)
                pool.wait_ge(za_b_copied, chunk + 1)
                pool.wait_ge(c_in, 32 * (chunk + 1))
                with pool.Fori(0, NB // 2) as i:
                    for p in range(2):
                        n = i * 2 + (chunk * NB + p)
                        h0 = i * (2 * HB) + p * HB
                        pool.wait_ge(block_done, n + 1)
                        pool.tensor_tensor(
                            v_t2[:, p].rearrange("q h (i j) -> q h i j", i=NI),
                            pim[:, :, bass.ds(h0, HB)].rearrange("q i h -> q h i").unsqueeze(3).to_broadcast([P, HB, NI, NJ]),
                            vj_b[:, :, bass.ds(h0, HB)].rearrange("q j h -> q h j").unsqueeze(2).to_broadcast([P, HB, NI, NJ]),
                            ALU.mult).then_inc(vt2_ready, 1)
                        pool.tensor_tensor(
                            w2[:, p, 0:HB // 2].rearrange("q h (c a) -> q h c a", c=BATCH),
                            cbuf[:, 1, bass.ds(h0, HB // 2), :].unsqueeze(3).to_broadcast([P, HB // 2, BATCH, NA]),
                            za_b_pool[:, :, bass.ds(h0, HB // 2)].rearrange("q a h -> q h a").unsqueeze(2).to_broadcast([P, HB // 2, BATCH, NA]),
                            ALU.mult).then_inc(w2_pool, 1)

        @block.scalar
        def _(act):
            def load_weights(n):
                act.dma_start(wraw[:, n % 2, :], weights[:, n * WCHUNK:(n + 1) * WCHUNK]).then_inc(wraw_in[n % 2], 16)

            def high_part(n):
                if n + 1 < NW:
                    if n >= 1:
                        act.wait_ge(wlo_ready, n)
                    load_weights(n + 1)
                act.wait_ge(wraw_in[n % 2], 16 * (n // 2 + 1))
                act.activation(whi[:, n * WCHUNK:(n + 1) * WCHUNK], wraw[:, n % 2, :], ACT.Copy).then_inc(whi_ready, 1)

            def magnitudes(chunk, k):
                x = dre[:, chunk * HC:(chunk + 1) * HC]
                for e, power in enumerate(EXPS[GROUPS[k]]):
                    ins = act.activation(mag[:, k, e, :], x, ACT.Exp, scale=float(power))
                if k == 0:
                    ins = act.activation(step_sc[:, 0, :], x, ACT.Tanh, scale=0.5)
                ins.then_inc(exps_ready, 1)

            act.sem_inc(y_out, 1)
            load_weights(0)
            for n in range(FIRST_SPLIT):
                high_part(n)
            act.wait_ge(consts_ready, 1)
            act.wait_ge(steps_ready, 1)
            for chunk in range(NCH):
                if chunk == 0:
                    magnitudes(chunk, 0)
                    magnitudes(chunk, 1)
                else:
                    act.wait_ge(tables_ready, chunk)
                magnitudes(chunk, 2)
                for k, name in enumerate(GROUPS):
                    n = chunk * 3 + k
                    act.wait_ge(angle_ready, n + 1)
                    if n >= 2:
                        act.wait_ge(scaled, n - 1)
                    if name == "p":
                        act.activation(im_t[:, n % 2], ang[:, n % 2], ACT.Sin).then_inc(sin_ready, 1)
                    else:
                        act.activation(im_t[lo, n % 2], ang[lo, n % 2], ACT.Sin, scale=-1.0)
                    if name == "j":
                        act.activation(step_sc[:, 1, :], ang[:, n % 2, 1, :], ACT.Sin)
                        act.activation(step_sc[:, 2, :], ang[:, n % 2, 1, :], ACT.Sin, scale=0.5).then_inc(half_ready, 1)
                    act.activation(kbuf[:, n % 2], ang[:, n % 2], ACT.Abs).then_inc(abs_ready, 1)
                    act.wait_ge(abs_ready, n + 1)
                    if n >= 1:
                        act.wait_ge(scaled, n)
                    if name == "p":
                        act.activation(re_t[:], kbuf[:, n % 2], ACT.Sin, scale=-1.0, bias=half_pi[:, 0:1]).then_inc(cos_ready, 1)
                    else:
                        act.activation(im_t[up, n % 2], kbuf[up, n % 2], ACT.Sin, scale=-1.0, bias=half_pi[up, 0:1]).then_inc(sin_ready, 1)
                        act.activation(re_t[lo], kbuf[lo, n % 2], ACT.Sin, scale=-1.0, bias=half_pi[lo, 0:1])
                        act.activation(re_t[up], ang[up, n % 2], ACT.Sin).then_inc(cos_ready, 1)
                    if FIRST_SPLIT + n < NW:
                        high_part(FIRST_SPLIT + n)
                if chunk + 1 < NCH:
                    act.wait_ge(scaled, chunk * 3 + 2)
                    act.wait_ge(g_ready, chunk + 1)
                    magnitudes(chunk + 1, 0)
                    magnitudes(chunk + 1, 1)
                else:
                    for n in range(FIRST_SPLIT + NCH * len(GROUPS), NW):
                        high_part(n)
                act.wait_ge(scaled, (chunk + 1) * len(GROUPS))
                act.activation(za_b_pool[:], za_b[:], ACT.Copy).then_inc(za_b_copied, 1)
                with act.Fori(0, NB // 2) as i:
                    for p in range(2):
                        n = i * 2 + (chunk * NB + p)
                        act.wait_ge(block_done, n + 3)
                        act.wait_ge(y_stored[p], i * 16 + chunk * NB * 8)
                        act.activation(ystage[:, p, :], ypsum[p][:], ACT.Copy).then_inc(y_out, 1)

        @block.vector
        def _(dve):
            link = dve_chain(dve, chain)
            dve.wait_ge(params_in, 16 * 5)
            x = logs[:].rearrange("q r h -> q (r h)")
            ck = ang[:, 0].rearrange("q e h -> q (e h)")[:, 0:2 * SEQ]
            cr = kbuf[:, 0].rearrange("q e h -> q (e h)")[:, 0:2 * SEQ]
            cp = re_t[:].rearrange("q e h -> q (e h)")[:, 0:2 * SEQ]
            link(dve.tensor_scalar(ck, x, LOG2E, MAGIC, ALU.mult, ALU.add))
            link(dve.tensor_scalar(ck, ck, MAGIC, None, ALU.subtract))
            link(dve.tensor_scalar(ck, ck, -126.0, 127.0, ALU.max, ALU.min))
            link(dve.scalar_tensor_tensor(out=cr, in0=ck, scalar=-LN2_HI, in1=x, op0=ALU.mult, op1=ALU.add))
            link(dve.scalar_tensor_tensor(out=cr, in0=ck, scalar=-LN2_LO, in1=cr, op0=ALU.mult, op1=ALU.add))
            factors = [1 / 5040, 1 / 720, 1 / 120, 1 / 24, 1 / 6, 1 / 2, 1.0]
            link(dve.tensor_scalar(cp, cr, factors[0], None, ALU.mult))
            for f in factors[1:]:
                link(dve.scalar_tensor_tensor(out=cp, in0=cp, scalar=f, in1=cr, op0=ALU.add, op1=ALU.mult))
            link(dve.tensor_scalar(cp, cp, 1.0, None, ALU.add))
            link(dve.tensor_scalar(ck.bitcast(I32), ck, 127.0, 2.0 ** 23, ALU.add, ALU.mult))
            link(dve.tensor_tensor(dtw[:].rearrange("q r h -> q (r h)"), cp, ck, ALU.mult))
            dve.scalar_tensor_tensor(out=dre[:], in0=dtw[:, 1, :], scalar=-1.0, in1=dtw[:, 0, :],
                                     op0=ALU.mult, op1=ALU.mult)
            dve.tensor_tensor(dim[:], wim[:], dtw[:, 0, :], ALU.mult).then_inc(steps_ready, 1)
            dve.wait_ge(steps_ready, 1)

            def reduce_angles(chunk, k):
                n = chunk * 3 + k
                a, kb = ang[:, n % 2], kbuf[:, n % 2]
                for e, power in enumerate(EXPS[GROUPS[k]]):
                    last = dve.tensor_scalar(a[:, e, :], dim[:, chunk * HC:(chunk + 1) * HC], float(power), None, ALU.mult)
                link(last)
                link(dve.tensor_scalar(kb, a, 1 / (2 * PI), MAGIC, ALU.mult, ALU.add))
                link(dve.tensor_scalar(kb, kb, MAGIC, None, ALU.subtract))
                link(dve.scalar_tensor_tensor(out=a, in0=kb, scalar=-C1, in1=a, op0=ALU.mult, op1=ALU.add))
                link(dve.scalar_tensor_tensor(out=a, in0=kb, scalar=-C2, in1=a, op0=ALU.mult, op1=ALU.add))
                dve.tensor_scalar(a, a, PI_BELOW, -PI_BELOW, ALU.min, ALU.max).then_inc(angle_ready, 1)

            for chunk in range(NCH):
                hs = slice(chunk * HC, (chunk + 1) * HC)
                if chunk:
                    dve.wait_ge(w2_pool, chunk * NB)
                reduce_angles(chunk, 0)
                if chunk == 0:
                    link(dve.tensor_tensor(inv2[:], dtw[:, 1, :], dtw[:, 1, :], ALU.mult))
                    link(dve.tensor_tensor(w_sq[:], wim[:], wim[:], ALU.mult))
                    link(dve.tensor_tensor(inv2[:], inv2[:], w_sq[:], ALU.add))
                    link(dve.reciprocal(w_sq[:], inv2[:]))
                    dve.tensor_scalar(inv2[lo], w_sq[lo], 2.0, None, ALU.mult)
                    dve.tensor_scalar(inv2[up], w_sq[up], -2.0, None, ALU.mult).then_inc(inv2_ready, 1)
                for k, name in enumerate(GROUPS):
                    n = chunk * 3 + k
                    if k + 1 < len(GROUPS):
                        reduce_angles(chunk, k + 1)
                    re, im = re_t[:], im_t[:, n % 2]
                    dve.wait_ge(exps_ready, n + 1)
                    dve.wait_ge(sin_ready, n + 1)
                    dve.wait_ge(cos_ready, n + 1)
                    if name == "p":
                        dve.tensor_tensor(pre[:], re, mag[:, k], ALU.mult)
                        dve.tensor_tensor(pim[:], im, mag[:, k], ALU.mult).then_inc(scaled, 1)
                        continue
                    if name == "j":
                        dve.tensor_tensor(vj_a[:], re, mag[:, k], ALU.mult)
                        dve.tensor_tensor(vj_b[:], im, mag[:, k], ALU.mult).then_inc(scaled, 1)
                        continue
                    dve.tensor_tensor(im, im, mag[:, k], ALU.mult)
                    link(dve.tensor_tensor(re, re, mag[:, k], ALU.mult))
                    dve.wait_ge(g_ready, chunk + 1)
                    t0, t1 = ang[:, n % 2], kbuf[:, n % 2]
                    gr, gi = g_re[:].to_broadcast([P, NA, HC]), g_im[:].to_broadcast([P, NA, HC])
                    dve.tensor_tensor(za_a[:], re, gr, ALU.mult)
                    dve.tensor_tensor(t0, im, gi, ALU.mult)
                    dve.tensor_tensor(za_b[:], im, gr, ALU.mult)
                    link(dve.tensor_tensor(t1, re, gi, ALU.mult))
                    dve.tensor_tensor(za_b[:], za_b[:], t1, ALU.subtract).then_inc(scaled, 1)
                    dve.tensor_tensor(za_a[:], za_a[:], t0, ALU.add).then_inc(tables_ready, 1)
                dve.wait_ge(tables_ready, chunk + 1)
                dve.wait_ge(za_b_copied, chunk + 1)
                dve.wait_ge(c_in, 32 * (chunk + 1))
                if chunk == 0:
                    dve.sem_inc(block_done, 2)
                with dve.Fori(0, NB // 2) as i:
                    for p in range(2):
                        n = i * 2 + (chunk * NB + p)
                        h0 = i * (2 * HB) + p * HB
                        dve.wait_ge(block_done, n + 1)
                        dve.tensor_tensor(
                            v_t1[:, p].rearrange("q h (i j) -> q h i j", i=NI),
                            pre[:, :, bass.ds(h0, HB)].rearrange("q i h -> q h i").unsqueeze(3).to_broadcast([P, HB, NI, NJ]),
                            vj_a[:, :, bass.ds(h0, HB)].rearrange("q j h -> q h j").unsqueeze(2).to_broadcast([P, HB, NI, NJ]),
                            ALU.mult).then_inc(vt1_ready, 1)
                        dve.tensor_tensor(
                            w1[:, p].rearrange("q h (c a) -> q h c a", c=BATCH),
                            cbuf[:, 0, bass.ds(h0, HB), :].unsqueeze(3).to_broadcast([P, HB, BATCH, NA]),
                            za_a[:, :, bass.ds(h0, HB)].rearrange("q a h -> q h a").unsqueeze(2).to_broadcast([P, HB, BATCH, NA]),
                            ALU.mult).then_inc(w1_ready, 1)
                        dve.tensor_tensor(
                            w2[:, p, HB // 2:].rearrange("q h (c a) -> q h c a", c=BATCH),
                            cbuf[:, 1, bass.ds(h0 + HB // 2, HB // 2), :].unsqueeze(3).to_broadcast([P, HB // 2, BATCH, NA]),
                            za_b[:, :, bass.ds(h0 + HB // 2, HB // 2)].rearrange("q a h -> q h a").unsqueeze(2).to_broadcast([P, HB // 2, BATCH, NA]),
                            ALU.mult).then_inc(w2_dve, 1)
                        dve.wait_ge(w2_dve, n + 1)
                        dve.tensor_tensor(w1[:, p, HB // 2:], w1[:, p, HB // 2:], w2[:, p, HB // 2:], ALU.add).then_inc(w_sum, 1)
                        dve.wait_ge(vt1_ready, n + 1)
                        dve.wait_ge(vt2_ready, n + 1)
                        dve.tensor_tensor(vblk[:, p], v_t1[:, p], v_t2[:, p], ALU.add).then_inc(v_ready, 1)
                dve.wait_ge(w2_dve, (chunk + 1) * NB)
                dve.wait_ge(w2_pool, (chunk + 1) * NB)
                dve.sem_inc(c_used, 1)

        @block.tensor
        def _(pe):
            for chunk in range(NCH):
                with pe.Fori(0, NB // 2) as i:
                    for p in range(2):
                        n = i * 2 + (chunk * NB + p)
                        pe.wait_ge(w1_ready, n + 1)
                        pe.wait_ge(w2_pool, n + 1)
                        pe.wait_ge(w_sum, n + 1)
                        pe.wait_ge(v_ready, n + 1)
                        pe.wait_ge(y_out, n)
                        for h in range(HB):
                            parts = (w1, w2) if h < HB // 2 else (w1,)
                            for k, w in enumerate(parts):
                                for rows in (lo, up):
                                    last = pe.matmul(ypsum[p][rows, h * NI * NJ:(h + 1) * NI * NJ], w[:, p, h, rows], vblk[:, p, h, :],
                                                     start=k == 0, stop=k == len(parts) - 1, tile_position=(0, rows.start))
                        last.then_inc(block_done, 1)


PT_ACT = (0, 1, 2, 4, 8, 9, 12, 13, 14, 15)
PT_LAG = 5
EARLY = 4
STEPS = HEADS + PT_LAG + 2
FILL = {
    4: [("QB", 0, 1), ("LOAD", 1, 0)],
    6: [("LNS", 1, 0)],
    7: [("LNR", 1, 0)],
    8: [("LNN", 1, 0)],
    10: [("XT", 1, 0)],
    11: [("XT", 1, 1)],
    13: [("QN", 1, 0)],
    14: [("CKV", 1, 0), ("KR", 1, 0)],
    16: [("QN", 1, 1)],
    17: [("QA", 1, 0)],
    18: [("QA", 1, 1)],
    20: [("V", 1, 0)],
    21: [("KRX", 1, 0)],
    22: [("KN", 1, 0), ("V", 1, 1)],
    STEPS: [("KN", 1, 1), ("WO", 0, 0), ("WO", 0, 1), ("LN2S", 0, 0)],
    STEPS + 1: [("LN2R", 0, 0), ("LN2N", 0, 0)],
    STEPS + 2: [("QB", 1, 0)],
    STEPS + 3: [("X2T", 0, 0), ("X2T", 0, 1)],
}


def attention_order(fill):
    def head_stages(step, ahead):
        before, after = [], []
        if step == 0:
            before.append(("QT", ahead, 0))
        if step % 2 == 1 and step < HEADS - 1:
            before.append(("QT", ahead, (step + 1) // 2))
        if 1 <= step <= HEADS:
            before.append(("S", ahead, step - 1))
        if 2 <= step <= HEADS + 1:
            before.append(("EXP", ahead, step - 2))
        if 3 <= step <= HEADS + 2:
            before.insert(0, ("REC", ahead, step - 3))
        if step >= PT_LAG + 5 and (step - PT_LAG - 1) % 4 == 0:
            after.append(("PV", ahead, (step - PT_LAG - 1) // 4 - 1))
        if PT_LAG + 1 <= step <= HEADS + PT_LAG:
            after.append(("PT", ahead, step - PT_LAG - 1))
        return before, after

    order = []
    for step in range(EARLY, STEPS + EARLY):
        before, after = head_stages(step, 0) if step < STEPS else head_stages(step - STEPS, 1)
        order += before + fill.get(step, []) + after
    return order


ORDER = attention_order(FILL)
FIRST = [(stage, 0, n) for stage, ahead, n in ORDER if ahead == 1]
LAST = [s for s in ORDER if s[1] == 0]
SHARED = ("XT", "CKV", "KR", "QN", "QA", "QB", "KN", "V", "WO", "X2T")


def attention(nc, mixed, whi, wlo, ident, rope_tok, rope_feat, causal, h2_dram, x2_dram):
    with ExitStack() as ctx:
        def sb(name, shape, dt=F32):
            return ctx.enter_context(nc.sbuf_tensor(name, shape, dt))

        def bank(name, shape):
            return ctx.enter_context(nc.psum_tensor(name, shape, F32))

        def sem(name):
            return ctx.enter_context(nc.semaphore(name))

        RING = 6
        mask = sb("mask", [P, 3 * P])
        cos_sin = sb("cos_sin", [P, 2, TT, ROPE])
        cos_sin_t = sb("cos_sin_t", [P, SEQ])
        h_sb = sb("h_sb", [P, 2, TT, DIM])
        xn = [sb(f"xn{j}", [P, TT, DIM]) for j in range(2)]
        stats = [sb(f"stats{j}", [P, TT, 6]) for j in range(2)]
        meanvar = [sb(f"meanvar{j}", [P, TT, 2]) for j in range(2)]
        lnt = [sb(f"lnt{j}", [P, 6, TT]) for j in range(2)]
        xt_hi = sb("xt_hi", [P, KD, SEQ], F32R)
        xt_lo = sb("xt_lo", [P, KD, SEQ], F32R)
        ck_hi = sb("ck_hi", [P, SEQ], F32R)
        ck_lo = sb("ck_lo", [P, SEQ], F32R)
        kr_a = sb("kr_a", [ROPE, SEQ])
        kr_b = sb("kr_b", [ROPE, SEQ])
        kr_s = sb("kr_s", [ROPE, SEQ])
        q_tok = sb("q_tok", [P, 2, TT, HEADS, DQK])
        q_rot = sb("q_rot", [P, 2, 8, ROPE])
        k_t = sb("k_t", [DQK, HEADS, SEQ])
        v_sb = sb("v_sb", [P, 2, TT, HEADS * DH])
        q_t = sb("q_t", [DQK, 2, 2, SEQ])
        probs = sb("probs", [P, RING, 3 * P])
        probs_t = sb("probs_t", [P, RING, 3 * P])
        neg_max = sb("neg_max", [P, HEADS, TT])
        sums = sb("sums", [P, HEADS, TT])
        recips = sb("recips", [P, HEADS, TT])
        o_hi = sb("o_hi", [P, KD, SEQ], F32R)
        o_lo = sb("o_lo", [P, KD, SEQ], F32R)
        x2_t = sb("x2_t", [P, KD, SEQ])

        shared = [bank(f"shared{i}", [P, 512]) for i in range(2)]
        qt_bank = bank("qt_bank", [DQK, 2, SEQ])
        s_bank = [bank(f"s_bank{i}", [P, 3 * P]) for i in range(2)]
        pt_bank = [bank(f"pt_bank{i}", [P, 3 * P]) for i in range(2)]
        pv_bank = bank("pv_bank", [P, SEQ])

        tables_in = sem("tables_in")
        h_in = [sem(f"h_in{i}") for i in range(2)]
        stat_done, var_ready, guess_ready, newton, xn_ready = (
            [sem(f"{n}{j}") for j in range(2)]
            for n in ("stat_done", "var_ready", "guess_ready", "newton", "xn_ready"))
        gates = {e: sem(f"gate_{e}") for e in ("sp", "pool", "dve")}
        done = {k: sem(f"done_{k}") for k in SHARED + ("QT", "S", "PT", "PV")}
        PER = {"XT": 2, "CKV": 1, "KR": 1, "QN": 2, "QA": 2, "QB": 2, "KN": 2, "V": 2, "WO": 2, "X2T": 2,
               "QT": 8, "S": HEADS, "PT": HEADS, "PV": 4}
        xt_hi_ready, xt_lo_ready, ck_hi_ready, ck_lo_ready, kr_read, kr_sum, kr_ready = map(
            sem, ("xt_hi_ready", "xt_lo_ready", "ck_hi_ready", "ck_lo_ready", "kr_read", "kr_sum", "kr_ready"))
        q_nope_ready, rope_read, q_rope_ready, kn_act, kn_dve, v_ready = map(
            sem, ("q_nope_ready", "rope_read", "q_rope_ready", "kn_act", "kn_dve", "v_ready"))
        qt_ready, max_ready, exp_ready, recip_ready, norm_ready, pt_act, pt_dve, o_hi_ready, o_lo_ready = map(
            sem, ("qt_ready", "max_ready", "exp_ready", "recip_ready", "norm_ready", "pt_act", "pt_dve",
                  "o_hi_ready", "o_lo_ready"))
        h2_ready, x2_ready, h2_stored, x2_stored = map(sem, ("h2_ready", "x2_ready", "h2_stored", "x2_stored"))

        def at(b, per, n):
            return b[0] * (2 * per) + (b[1] * per + n)

        def wait(eng, s, b, per, n):
            value = at(b, per, n)
            if not isinstance(value, int) or value > 0:
                eng.wait_ge(s, value)

        FREES = {"XT": [(xt_lo_ready, 2)], "CKV": [(ck_lo_ready, 1)], "KR": [(kr_read, 1)],
                 "QN": [(q_nope_ready, 2)], "QA": [(rope_read, 4)], "QB": [(rope_read, 4)],
                 "KN": [(kn_act, 2), (kn_dve, 2)], "V": [(v_ready, 2)], "WO": [(h2_ready, 2)], "X2T": [(x2_ready, 2)]}

        LAST_USES = {stage: (ahead, n) for stage, ahead, n in
                     [s for s in ORDER if s[0] in SHARED][-2:] + [(s, 1, n) for s, _, n in FIRST if s in SHARED][-2:]}

        def gate(eng, name):
            eng.sem_inc(gates[name], 1)

        def walk(eng, stages):
            stages(FIRST, (0, 0), True)
            with eng.Fori(0, BATCH // 2 - 1) as i:
                stages(ORDER, (i, 0), False)
                stages(ORDER, (i, 1), False)
            stages(ORDER, (BATCH // 2 - 1, 0), False)
            stages(LAST, (BATCH // 2 - 1, 1), False)

        block = ctx.enter_context(nc.Block())

        @block.sync
        def _(sp):
            def rows(b, t):
                return bass.ds(b[0] * (2 * SEQ) + (b[1] * SEQ + t * P), P)

            def stages(order, base, first):
                for stage, ahead, n in order:
                    b = (base[0], base[1] + ahead)
                    if stage == "LOAD":
                        wait(sp, h2_stored, b, 16, -16)
                        gate(sp, "sp")
                        wait(sp, xn_ready[1], b, 2, -2)
                        gate(sp, "sp")
                        for t in range(TT):
                            src = mixed.rearrange("(c a) h l -> c h a l", a=NA)
                            src = src[bass.ds(b[0] * 2 + b[1], 1), t * P:(t + 1) * P, :, :].rearrange("c h a l -> (c h) a l")
                            sp.dma_start(h_sb[:, b[1] % 2, t, :].rearrange("q (a l) -> q a l", a=NA), src
                                         ).then_inc(h_in[b[1] % 2], 16)
                    if stage == "LN2S":
                        wait(sp, h2_ready, b, 2, 2)
                        gate(sp, "sp")
                        sp.dma_start(h2_dram[bass.ds(b[0] * (2 * SEQ) + b[1] * SEQ, SEQ), :].rearrange("(t q) d -> q t d", q=P),
                                     h_sb[:, b[1] % 2]).then_inc(h2_stored, 16)
                    if stage == "X2T" and n == 1:
                        wait(sp, x2_ready, b, 2, 2)
                        gate(sp, "sp")
                        sp.dma_start(x2_dram[:, :, bass.ds(b[0] * (2 * SEQ) + b[1] * SEQ, SEQ)], x2_t[:]).then_inc(x2_stored, 16)

            walk(sp, stages)
            sp.wait_ge(h2_stored, 16 * BATCH)
            sp.wait_ge(x2_stored, 16 * BATCH)

        @block.gpsimd
        def _(pool):
            def normalise(j, b):
                wait(pool, newton[j], b, 5, 5)
                wait(pool, done["XT" if j == 0 else "X2T"], b, 2, 0)
                gate(pool, "pool")
                for t in range(TT):
                    pool.tensor_scalar(xn[j][:, t, :], h_sb[:, b[1] % 2, t, :], lnt[j][:, 4, t:t + 1],
                                       lnt[j][:, 5, t:t + 1], ALU.mult, ALU.add).then_inc(xn_ready[j], 1)

            def add_rope(part, b, t):
                wait(pool, rope_read, b, 4, 2 * part + t + 1)
                q = q_tok[:, b[1] % 2, t, 8 * part:8 * part + 8, 0:ROPE]
                pool.tensor_tensor(q, q, q_rot[:, t], ALU.add).then_inc(q_rope_ready, 1)

            def stages(order, base, first):
                for stage, ahead, n in order:
                    b = (base[0], base[1] + ahead)
                    if stage == "LNN":
                        normalise(0, b)
                    if stage == "LN2N":
                        normalise(1, b)
                    if stage == "QA":
                        add_rope(0, b, n)
                    if stage == "QB":
                        add_rope(1, b, n)
                    if stage == "REC":
                        wait(pool, recip_ready, b, HEADS, n + 1)
                        gate(pool, "pool")
                        for t, cols in enumerate((slice(0, P), slice(P, 3 * P))):
                            ins = pool.tensor_scalar(probs[:, n % RING, cols], probs[:, n % RING, cols],
                                                     recips[:, n, t:t + 1], 1.0, ALU.mult, ALU.mult)
                        ins.then_inc(norm_ready, 1)
                    if stage == "KRX":
                        wait(pool, kr_read, b, 1, 1)
                        pool.tensor_tensor(kr_s[:], kr_a[:], kr_b[:], ALU.add).then_inc(kr_sum, 1)
                        wait(pool, kr_sum, b, 1, 1)
                        wait(pool, done["S"], b, HEADS, 0)
                        gate(pool, "pool")
                        pool.tensor_scalar(k_t[0:ROPE, :, :], kr_s[:].unsqueeze(1).to_broadcast([ROPE, HEADS, SEQ]),
                                           1.0, 0.0, ALU.mult, ALU.add).then_inc(kr_ready, 1)

            walk(pool, stages)

        @block.scalar
        def _(act):
            act.dma_start(mask[:], causal).then_inc(tables_in, 16)
            act.dma_start(cos_sin[:], rope_tok).then_inc(tables_in, 16)
            act.dma_start(cos_sin_t[:], rope_feat).then_inc(tables_in, 16)
            act.preload_act_table_set("natural_log_exp_and_others")
            act.wait_ge(tables_in, 48)

            def guess(j, b):
                wait(act, var_ready[j], b, 1, 1)
                act.activation(lnt[j][:, 1, :], lnt[j][:, 0, :], ACT.Ln).then_inc(guess_ready[j], 1)
                wait(act, guess_ready[j], b, 2, 1)
                act.activation(lnt[j][:, 2, :], lnt[j][:, 1, :], ACT.Exp, scale=-0.5).then_inc(guess_ready[j], 1)

            def stages(order, base, first):
                use = 0
                for stage, ahead, n in order:
                    b = (base[0], base[1] + ahead)
                    half = b[1] % 2
                    ps = shared[use % 2]
                    use += stage in SHARED
                    if stage == "LNR":
                        guess(0, b)
                    if stage == "LN2R":
                        guess(1, b)
                    if stage == "XT":
                        wait(act, done["XT"], b, 2, n + 1)
                        wait(act, done["QB"], b, 2, 0)
                        act.activation(xt_hi[:, :, n * P:(n + 1) * P], ps[:].rearrange("q (k s) -> q k s", k=KD),
                                       ACT.Copy).then_inc(xt_hi_ready, 1)
                    if stage == "CKV":
                        wait(act, done["CKV"], b, 1, 1)
                        wait(act, done["V"], b, 2, 0)
                        wait(act, done["KN"], b, 2, 0)
                        act.activation(ck_hi[:], ps[:, 0:SEQ], ACT.Copy).then_inc(ck_hi_ready, 1)
                    if stage == "QN":
                        wait(act, done["QN"], b, 2, n + 1)
                        wait(act, done["QT"], b, 8, -8)
                        act.activation(q_tok[:, half, n, :, ROPE:DQK], ps[:].rearrange("q (h d) -> q h d", h=HEADS),
                                       ACT.Copy).then_inc(q_nope_ready, 1)
                    if stage == "KN":
                        wait(act, done["KN"], b, 2, n + 1)
                        wait(act, done["S"], b, HEADS, 0)
                        for j in range(2):
                            ins = act.activation(k_t[ROPE:DQK, 8 * n + j:8 * n + j + 5:4, :],
                                                 ps[32 * j:32 * j + 32, :].rearrange("q (g s) -> q g s", g=2), ACT.Copy)
                        ins.then_inc(kn_act, 1)
                    if stage == "V":
                        wait(act, done["V"], b, 2, n + 1)
                        wait(act, done["PV"], b, 4, -4)
                        act.activation(v_sb[:, half, n, :], ps[:], ACT.Copy).then_inc(v_ready, 1)
                    if stage == "X2T":
                        wait(act, done["X2T"], b, 2, n + 1)
                        wait(act, x2_stored, b, 16, 0)
                        act.activation(x2_t[:, :, n * P:(n + 1) * P], ps[:].rearrange("q (k s) -> q k s", k=KD),
                                       ACT.Copy).then_inc(x2_ready, 1)
                    if stage == "QT":
                        wait(act, done["QT"], b, 8, n + 1)
                        wait(act, done["S"], b, HEADS, 2 * n - 2 if n >= 2 else 0)
                        act.activation(q_t[:, n % 2], qt_bank[:], ACT.Copy).then_inc(qt_ready, 1)
                    if stage == "EXP":
                        wait(act, max_ready, b, HEADS, n + 1)
                        for t, cols in enumerate((slice(0, P), slice(P, 3 * P))):
                            ins = act.activation(probs[:, n % RING, cols], probs[:, n % RING, cols], ACT.Exp,
                                                 bias=neg_max[:, n, t:t + 1], scale=-1.0, accum_out=sums[:, n, t:t + 1])
                        ins.then_inc(exp_ready, 1)
                    if stage == "PT" and n in PT_ACT:
                        wait(act, done["PT"], b, HEADS, n + 1)
                        wait(act, done["PV"], b, 4, (n - RING) // 4 + 1 if n >= RING else 0)
                        act.activation(probs_t[:, n % RING, :], pt_bank[n % 2][:], ACT.Copy).then_inc(pt_act, 1)
                    if stage == "PV":
                        wait(act, done["PV"], b, 4, n + 1)
                        wait(act, done["WO"], b, 2, 0)
                        act.activation(o_hi[:, n, :], pv_bank[:], ACT.Copy).then_inc(o_hi_ready, 1)

            walk(act, stages)

        @block.vector
        def _(dve):
            dve.wait_ge(tables_in, 48)

            def statistics(j, b):
                h = h_sb[:, b[1] % 2]
                wait(dve, xn_ready[j], b, 2, 0)
                if j == 0:
                    dve.wait_ge(h_in[b[1] % 2], b[0] * 32 + (b[1] // 2 * 32 + 32))
                else:
                    wait(dve, h2_ready, b, 2, 2)
                for t in range(TT):
                    dve.bn_stats(stats[j][:, t, :], h[:, t, :]).then_inc(stat_done[j], 1)
                wait(dve, stat_done[j], b, 4, 2)
                gate(dve, "dve")
                for t in range(TT):
                    dve.bn_aggr(meanvar[j][:, t, :], stats[j][:, t, :]).then_inc(stat_done[j], 1)
                wait(dve, stat_done[j], b, 4, 4)
                dve.tensor_scalar(lnt[j][:, 0, :], meanvar[j][:, :, 1], EPS, None, ALU.add).then_inc(var_ready[j], 1)

            def newton_step(j, b):
                v, g, s, y, m = (lnt[j][:, k, :] for k in (0, 2, 3, 4, 5))
                wait(dve, guess_ready[j], b, 2, 2)
                dve.tensor_tensor(s, g, g, ALU.mult).then_inc(newton[j], 1)
                wait(dve, newton[j], b, 5, 1)
                dve.tensor_tensor(s, s, v, ALU.mult).then_inc(newton[j], 1)
                wait(dve, newton[j], b, 5, 2)
                dve.tensor_scalar(s, s, -0.5, 1.5, ALU.mult, ALU.add).then_inc(newton[j], 1)
                wait(dve, newton[j], b, 5, 3)
                dve.tensor_tensor(y, g, s, ALU.mult).then_inc(newton[j], 1)
                wait(dve, newton[j], b, 5, 4)
                dve.scalar_tensor_tensor(out=m, in0=meanvar[j][:, :, 0], scalar=-1.0, in1=y,
                                         op0=ALU.mult, op1=ALU.mult).then_inc(newton[j], 1)

            def rotate(part, b, t, ps):
                x = ps[:].rearrange("q (h d) -> q h d", h=8)
                r = 2 * part + t
                wait(dve, done["QA" if part == 0 else "QB"], b, 2, t + 1)
                if part == 0:
                    wait(dve, done["QT"], b, 8, -8)
                wait(dve, q_rope_ready, b, 4, r - 1 if r >= 2 else 0)
                dve.tensor_tensor(q_tok[:, b[1] % 2, t, 8 * part:8 * part + 8, 0:ROPE], x,
                                  cos_sin[:, 0, t, :].unsqueeze(1).to_broadcast([P, 8, ROPE]), ALU.mult)
                dve.tensor_tensor(q_rot[:, t].rearrange("q h (a d) -> q h a d", a=2),
                                  x.rearrange("q h (a d) -> q h a d", a=2)[:, :, ::-1, :],
                                  cos_sin[:, 1, t, :].rearrange("q (a d) -> q a d", a=2).unsqueeze(1).to_broadcast([P, 8, 2, ROPE // 2]),
                                  ALU.mult).then_inc(rope_read, 1)

            def stages(order, base, first):
                use = 0
                for stage, ahead, n in order:
                    b = (base[0], base[1] + ahead)
                    ps = shared[use % 2]
                    use += stage in SHARED
                    if stage == "LNS":
                        statistics(0, b)
                    if stage == "LN2S":
                        statistics(1, b)
                    if stage == "LNN":
                        newton_step(0, b)
                    if stage == "LN2N":
                        newton_step(1, b)
                    if stage == "XT":
                        wait(dve, xt_hi_ready, b, 2, n + 1)
                        dve.tensor_tensor(xt_lo[:, :, n * P:(n + 1) * P], ps[:].rearrange("q (k s) -> q k s", k=KD),
                                          xt_hi[:, :, n * P:(n + 1) * P].bitcast(F32), ALU.subtract).then_inc(xt_lo_ready, 1)
                    if stage == "CKV":
                        wait(dve, ck_hi_ready, b, 1, 1)
                        dve.tensor_tensor(ck_lo[:], ps[:, 0:SEQ], ck_hi[:].bitcast(F32), ALU.subtract).then_inc(ck_lo_ready, 1)
                    if stage == "KR":
                        wait(dve, done["KR"], b, 1, 1)
                        wait(dve, kr_sum, b, 1, 0)
                        dve.tensor_tensor(kr_a[:], ps[0:ROPE, 0:SEQ], cos_sin_t[0:ROPE, :], ALU.mult)
                        dve.tensor_tensor(kr_b[:], ps[ROPE:P, 0:SEQ], cos_sin_t[ROPE:P, :], ALU.mult).then_inc(kr_read, 1)
                    if stage == "QA":
                        rotate(0, b, n, ps)
                    if stage == "QB":
                        rotate(1, b, n, ps)
                    if stage == "KN":
                        wait(dve, done["KN"], b, 2, n + 1)
                        wait(dve, done["S"], b, HEADS, 0)
                        for j in range(2, 4):
                            ins = dve.tensor_copy(k_t[ROPE:DQK, 8 * n + j:8 * n + j + 5:4, :],
                                                  ps[32 * j:32 * j + 32, :].rearrange("q (g s) -> q g s", g=2))
                        ins.then_inc(kn_dve, 1)
                    if stage == "WO":
                        wait(dve, done["WO"], b, 2, n + 1)
                        h = h_sb[:, b[1] % 2, n, :]
                        dve.tensor_tensor(h, ps[:], h, ALU.add).then_inc(h2_ready, 1)
                    if stage == "S":
                        wait(dve, done["S"], b, HEADS, n + 1)
                        wait(dve, done["PT"], b, HEADS, n - RING + 1 if n >= RING else 0)
                        gate(dve, "dve")
                        for t, cols in enumerate((slice(0, P), slice(P, 3 * P))):
                            ins = dve.tensor_tensor_reduce(probs[:, n % RING, cols], s_bank[n % 2][:, cols], mask[:, cols],
                                                           -SCALE, 3.0e38, ALU.add, ALU.min, neg_max[:, n, t:t + 1])
                        ins.then_inc(max_ready, 1)
                    if stage == "REC":
                        wait(dve, exp_ready, b, HEADS, n + 1)
                        dve.reciprocal(recips[:, n, :], sums[:, n, :]).then_inc(recip_ready, 1)
                    if stage == "PT" and n not in PT_ACT:
                        wait(dve, done["PT"], b, HEADS, n + 1)
                        wait(dve, done["PV"], b, 4, (n - RING) // 4 + 1 if n >= RING else 0)
                        dve.tensor_copy(probs_t[:, n % RING, :], pt_bank[n % 2][:]).then_inc(pt_dve, 1)
                    if stage == "PV":
                        wait(dve, o_hi_ready, b, 4, n + 1)
                        dve.tensor_tensor(o_lo[:, n, :], pv_bank[:], o_hi[:, n, :].bitcast(F32),
                                          ALU.subtract).then_inc(o_lo_ready, 1)

            walk(dve, stages)

        @block.tensor
        def _(pe):
            pe.wait_ge(tables_in, 48)

            def three(out, pairs, width=None):
                for n, ((lh, ll), (rh, rl)) in enumerate(pairs):
                    pe.matmul(out, lh, rh, start=n == 0, stop=False)
                    pe.matmul(out, lh, rl, start=False, stop=False)
                    last = pe.matmul(out, ll, rh, start=False, stop=n == len(pairs) - 1)
                return last

            def weight(col, width):
                return whi[:, col:col + width], wlo[:, col:col + width]

            def x_of(k, cols):
                return xt_hi[:, k, cols], xt_lo[:, k, cols]

            def pt_copied(b, h):
                copies = sum(x <= h for x in PT_ACT)
                wait(pe, pt_act, b, len(PT_ACT), copies)
                wait(pe, pt_dve, b, HEADS - len(PT_ACT), h + 1 - copies)

            def stages(order, base, first):
                uses = [s for s in order if s[0] in SHARED]
                use = 0
                for stage, ahead, n in order:
                    b = (base[0], base[1] + ahead)
                    half = b[1] % 2
                    tile = slice(n * P, (n + 1) * P)
                    if stage in SHARED:
                        ps = shared[use % 2]
                        if use >= 2:
                            was, ahead_was, n_was = uses[use - 2]
                            b_was = (base[0], base[1] + ahead_was)
                            for s, per in FREES[was]:
                                wait(pe, s, b_was, per, n_was + 1 + (2 if was == "QB" else 0))
                        elif not first:
                            for was, (ahead_was, n_was) in LAST_USES.items():
                                for s, per in FREES[was]:
                                    wait(pe, s, (base[0], base[1] + ahead_was - 1), per, n_was + 1 + (2 if was == "QB" else 0))
                        use += 1
                    if stage in ("XT", "X2T"):
                        j = 0 if stage == "XT" else 1
                        wait(pe, xn_ready[j], b, 2, n + 1)
                        for k in range(KD):
                            last = pe.transpose(ps[:, k * P:(k + 1) * P], xn[j][:, n, k * P:(k + 1) * P], ident[:])
                    if stage == "CKV":
                        wait(pe, xt_lo_ready, b, 2, 2)
                        last = three(ps[:, 0:SEQ], [(weight(WDKV + k * LATENT, LATENT), x_of(k, slice(0, SEQ))) for k in range(KD)])
                    if stage == "KR":
                        last = three(ps[:, 0:SEQ], [(weight(WKR + k * 2 * ROPE, 2 * ROPE), x_of(k, slice(0, SEQ))) for k in range(KD)])
                    if stage in ("QN", "QA", "QB"):
                        col = WQ + ("QN", "QA", "QB").index(stage) * 512
                        last = three(ps[:], [(x_of(k, tile), weight(col + k * HEADS * DQK, 512)) for k in range(KD)])
                    if stage == "KN":
                        wait(pe, ck_lo_ready, b, 1, 1)
                        for g in range(2):
                            last = three(ps[:, g * SEQ:(g + 1) * SEQ],
                                         [(weight(WUK + (2 * n + g) * P, P), (ck_hi[:], ck_lo[:]))])
                    if stage == "V":
                        wait(pe, ck_lo_ready, b, 1, 1)
                        last = three(ps[:], [((ck_hi[:, tile], ck_lo[:, tile]), weight(WUV, 512))])
                    if stage == "WO":
                        wait(pe, o_lo_ready, b, 4, 4)
                        last = three(ps[:], [((o_hi[:, g, tile], o_lo[:, g, tile]), weight(WO + g * DIM, DIM)) for g in range(KD)])
                    if stage == "QT":
                        if n == 0:
                            wait(pe, q_nope_ready, b, 2, 2)
                        if n in (0, 4):
                            wait(pe, q_rope_ready, b, 4, 2 if n == 0 else 4)
                        wait(pe, qt_ready, b, 8, n)
                        for h in range(2):
                            for t in range(TT):
                                last = pe.transpose(qt_bank[:, h, t * P:(t + 1) * P], q_tok[:, half, t, 2 * n + h, :], ident[:])
                    if stage == "S":
                        if n == 0:
                            wait(pe, kn_act, b, 2, 2)
                            wait(pe, kn_dve, b, 2, 2)
                            wait(pe, kr_ready, b, 1, 1)
                        wait(pe, qt_ready, b, 8, n // 2 + 1)
                        wait(pe, max_ready, b, HEADS, n - 1 if n >= 2 else 0)
                        q = q_t[:, n // 2 % 2, n % 2, :]
                        pe.matmul(s_bank[n % 2][:, 0:P], q[:, 0:P], k_t[:, n, 0:P], start=True, stop=True)
                        last = pe.matmul(s_bank[n % 2][:, P:3 * P], q[:, P:SEQ], k_t[:, n, :], start=True, stop=True)
                    if stage == "PT":
                        wait(pe, norm_ready, b, HEADS, n + 1)
                        if n >= 2:
                            pt_copied(b, n - 2)
                        else:
                            pt_copied(b, -1)
                        for k in range(3):
                            last = pe.transpose(pt_bank[n % 2][:, k * P:(k + 1) * P], probs[:, n % RING, k * P:(k + 1) * P], ident[:])
                    if stage == "PV":
                        pt_copied(b, 4 * n + 3)
                        wait(pe, v_ready, b, 2, 2)
                        wait(pe, o_lo_ready, b, 4, n)
                        for k, (src, dst) in enumerate(((slice(0, SEQ), slice(0, SEQ)), (slice(SEQ, SEQ + P), slice(P, SEQ)))):
                            for j in range(4):
                                h = 4 * n + j
                                last = pe.matmul(pv_bank[32 * j:32 * j + 32, dst], v_sb[:, half, k, h * DH:(h + 1) * DH],
                                                 probs_t[:, h % RING, src], start=k == 0, stop=k == 1, tile_position=(0, 32 * j))
                    if stage in done:
                        last.then_inc(done[stage], 1)

            walk(pe, stages)


def feed_forward(nc, x2_dram, h2_dram, w_up, w_down, bias_up, bias_down, out):
    with ExitStack() as ctx:
        def sb(name, shape, dt=F32):
            return ctx.enter_context(nc.sbuf_tensor(name, shape, dt))

        def bank(name, shape):
            return ctx.enter_context(nc.psum_tensor(name, shape, F32))

        def sem(name):
            return ctx.enter_context(nc.semaphore(name))

        CH = 512
        NC = TOKENS // CH
        NT = CH // P
        NM = HIDDEN // P
        RAW = 3
        G = 3
        up_hi = sb("up_hi", [P, NM, KD, P], F32R)
        up_lo = sb("up_lo", [P, NM, KD, P], F32R)
        down_hi = sb("down_hi", [P, NM, DIM], F32R)
        down_lo = sb("down_lo", [P, NM, DIM], F32R)
        raw = sb("raw", [P, RAW, 2, DIM])
        b1 = sb("b1", [P, NM])
        b2 = sb("b2", [P, DIM])
        x_raw = sb("x_raw", [P, KD, CH])
        x_hi = sb("x_hi", [P, KD, CH], F32R)
        x_lo = sb("x_lo", [P, KD, CH], F32R)
        g_raw = sb("g_raw", [P, 2, CH])
        g_hi = sb("g_hi", [P, G, CH], F32R)
        g_lo = sb("g_lo", [P, G, CH], F32R)
        res = sb("res", [P, NT, DIM])
        up_bank = [bank(f"up_bank{i}", [P, CH]) for i in range(2)]
        out_bank = [bank(f"out_bank{i}", [P, DIM]) for i in range(NT)]

        raw_in = [[sem(f"raw_{part}_in{i}") for part in ("up", "down")] for i in range(RAW)]
        x_in = [sem(f"x_in{k}") for k in range(KD)]
        bias_in, res_in, w_ready, w_half = map(sem, ("bias_in", "res_in", "w_ready", "w_half"))
        x_hi_ready, x_lo_ready, up_done, gelu_done, g_hi_ready, g_lo_ready = map(
            sem, ("x_hi_ready", "x_lo_ready", "up_done", "gelu_done", "g_hi_ready", "g_lo_ready"))
        down_done, res_biased, out_ready, out_stored, gate_sp = map(
            sem, ("down_done", "res_biased", "out_ready", "out_stored", "gate_sp"))
        block = ctx.enter_context(nc.Block())

        @block.sync
        def _(sp):
            def load_x(c):
                sp.wait_ge(x_lo_ready, c * KD)
                sp.sem_inc(gate_sp, 1)
                for k in range(KD):
                    sp.dma_start(x_raw[:, k, :], x2_dram[:, k, bass.ds(c * CH, CH)]).then_inc(x_in[k], 16)

            def load_res(c):
                sp.wait_ge(out_stored, c * (16 * NT))
                sp.sem_inc(gate_sp, 1)
                sp.dma_start(res[:], h2_dram[bass.ds(c * CH, CH), :].rearrange("(t q) d -> q t d", q=P)).then_inc(res_in, 16)

            def store(c):
                for t in range(NT):
                    sp.wait_ge(out_ready, c * NT + (t + 1))
                    sp.sem_inc(gate_sp, 1)
                    sp.dma_start(out[bass.ds(c * CH + t * P, P), :], res[:, t, :]).then_inc(out_stored, 16)

            for k in range(KD):
                sp.dma_start(x_raw[:, k, :], x2_dram[:, k, 0:CH]).then_inc(x_in[k], 16)
            for m in range(1, NM):
                if m >= RAW:
                    sp.wait_ge(w_ready, 2 * (m - RAW) + 2)
                sp.dma_start(raw[:, m % RAW, 0, :], w_up[:, m, :]).then_inc(raw_in[m % RAW][0], 16)
                sp.dma_start(raw[:, m % RAW, 1, :], w_down[:, m, :]).then_inc(raw_in[m % RAW][1], 16)
                if m == 1:
                    sp.dma_start(b1[:], bias_up).then_inc(bias_in, 16)
                    sp.dma_start(b2[:], bias_down.rearrange("(a d) -> a d", a=1).to_broadcast([P, DIM])).then_inc(bias_in, 16)
            with sp.Fori(0, NC - 1) as c:
                load_res(c)
                load_x(c + 1)
                store(c)
            load_res(NC - 1)
            store(NC - 1)
            sp.wait_ge(out_stored, 16 * NT * NC)

        def split_x(eng, c):
            for k in range(KD):
                eng.wait_ge(x_hi_ready, c * KD + (k + 1))
                eng.tensor_tensor(x_lo[:, k, :], x_raw[:, k, :], x_hi[:, k, :].bitcast(F32),
                                  ALU.subtract).then_inc(x_lo_ready, 1)

        @block.gpsimd
        def _(pool):
            def add_bias(c):
                pool.wait_ge(res_in, c * 16 + 16)
                for t in range(NT):
                    pool.tensor_tensor(res[:, t, :], res[:, t, :], b2[:], ALU.add).then_inc(res_biased, 1)

            for m in range(NM):
                for part, (hi, lo) in enumerate(((up_hi[:, m].rearrange("q k j -> q (k j)"), up_lo[:, m].rearrange("q k j -> q (k j)")),
                                                 (down_hi[:, m, :], down_lo[:, m, :]))):
                    pool.wait_ge(raw_in[m % RAW][part], 16 * (m // RAW + 1))
                    pool.tensor_scalar(hi, raw[:, m % RAW, part, :], 1.0, 1.0, ALU.mult, ALU.mult).then_inc(w_half, 1)
                    pool.wait_ge(w_half, 2 * m + part + 1)
                    pool.tensor_tensor(lo, raw[:, m % RAW, part, :], hi.bitcast(F32), ALU.subtract).then_inc(w_ready, 1)
            pool.wait_ge(bias_in, 32)
            add_bias(0)
            with pool.Fori(1, NC) as c:
                split_x(pool, c)
                add_bias(c)

        @block.scalar
        def _(act):
            act.dma_start(raw[:, 0, 0, :], w_up[:, 0, :]).then_inc(raw_in[0][0], 16)
            act.dma_start(raw[:, 0, 1, :], w_down[:, 0, :]).then_inc(raw_in[0][1], 16)
            with act.Fori(0, NC) as c:
                act.wait_ge(up_done, c * NM)
                for k in range(KD):
                    act.wait_ge(x_in[k], c * 16 + 16)
                    act.activation(x_hi[:, k, :], x_raw[:, k, :], ACT.Copy).then_inc(x_hi_ready, 1)
                act.wait_ge(bias_in, 32)
                for m in range(NM):
                    act.wait_ge(up_done, c * NM + (m + 1))
                    act.wait_ge(g_lo_ready, c * NM + (m - 1 if m >= 2 else 0))
                    act.activation(g_raw[:, m % 2, :], up_bank[m % 2][:], ACT.Gelu, bias=b1[:, m:m + 1]).then_inc(gelu_done, 1)
                    act.wait_ge(gelu_done, c * NM + (m + 1))
                    act.wait_ge(down_done, c * NM + (m - G + 1 if m >= G else 0))
                    act.activation(g_hi[:, m % G, :], g_raw[:, m % 2, :], ACT.Copy).then_inc(g_hi_ready, 1)

        @block.vector
        def _(dve):
            split_x(dve, 0)
            with dve.Fori(0, NC) as c:
                for m in range(NM):
                    dve.wait_ge(g_hi_ready, c * NM + (m + 1))
                    dve.tensor_tensor(g_lo[:, m % G, :], g_raw[:, m % 2, :], g_hi[:, m % G, :].bitcast(F32),
                                      ALU.subtract).then_inc(g_lo_ready, 1)
                dve.wait_ge(down_done, c * NM + NM)
                for t in range(NT):
                    dve.wait_ge(res_biased, c * NT + (t + 1))
                    dve.tensor_tensor(res[:, t, :], out_bank[t][:], res[:, t, :], ALU.add).then_inc(out_ready, 1)

        @block.tensor
        def _(pe):
            def up(c, m):
                if m < 2:
                    pe.wait_ge(gelu_done, c * NM)
                else:
                    pe.wait_ge(gelu_done, c * NM + (m - 1))
                pe.wait_ge(w_ready, 2 * m + 1)
                for k in range(KD):
                    if m == 0:
                        pe.wait_ge(x_lo_ready, c * KD + (k + 1))
                    pe.matmul(up_bank[m % 2][:], up_hi[:, m, k, :], x_hi[:, k, :], start=k == 0, stop=False)
                    pe.matmul(up_bank[m % 2][:], up_hi[:, m, k, :], x_lo[:, k, :], start=False, stop=False)
                    last = pe.matmul(up_bank[m % 2][:], up_lo[:, m, k, :], x_hi[:, k, :], start=False, stop=k == KD - 1)
                last.then_inc(up_done, 1)

            def down(c, m):
                pe.wait_ge(g_lo_ready, c * NM + (m + 1))
                pe.wait_ge(w_ready, 2 * m + 2)
                if m == 0:
                    pe.wait_ge(out_ready, c * NT)
                for t in range(NT):
                    rows = slice(t * P, (t + 1) * P)
                    pe.matmul(out_bank[t][:], g_hi[:, m % G, rows], down_hi[:, m, :], start=m == 0, stop=False)
                    pe.matmul(out_bank[t][:], g_hi[:, m % G, rows], down_lo[:, m, :], start=False, stop=False)
                    last = pe.matmul(out_bank[t][:], g_lo[:, m % G, rows], down_hi[:, m, :], start=False, stop=m == NM - 1)
                last.then_inc(down_done, 1)

            with pe.Fori(0, NC) as c:
                for m in range(NM):
                    up(c, m)
                    if m >= 2:
                        down(c, m - 2)
                down(c, NM - 2)
                down(c, NM - 1)


def vit_layer(nc, c_parts, log_dt, log_w_real, w_imag, weights, rope_tok, rope_feat, causal,
              w_up, w_down, bias_up, bias_down, out):
    assert SEQ == TT * P and DIM == KD * P and HEADS * DH == DIM and NA * NI * NJ == DIM
    mixed = nc.dram_tensor("mixed", [P, SEQ, NI * NJ], F32).ap()
    h2_dram = nc.dram_tensor("h2_dram", [TOKENS, DIM], F32).ap()
    x2_dram = nc.dram_tensor("x2_dram", [P, KD, TOKENS], F32).ap()
    with ExitStack() as ctx:
        whi = ctx.enter_context(nc.sbuf_tensor("whi", [P, WCOLS], F32R))
        wlo = ctx.enter_context(nc.sbuf_tensor("wlo", [P, WCOLS], F32R))
        ident = ctx.enter_context(nc.sbuf_tensor("ident", [P, P], F32))
        token_mixer(nc, c_parts, log_dt, log_w_real, w_imag, weights, whi, wlo, ident, mixed)
        attention(nc, mixed, whi, wlo, ident, rope_tok, rope_feat, causal, h2_dram, x2_dram)
    feed_forward(nc, x2_dram, h2_dram, w_up, w_down, bias_up, bias_down, out)


def kernel(x, L0_tok_log_dt, L0_tok_log_w_real, L0_tok_w_imag, L0_attn_Wq, L0_attn_Wdkv, L0_attn_Wkr, L0_attn_Wukv,
           L0_attn_Wo, L0_ffn_proj1, L0_ffn_proj1_bias, L0_ffn_proj2, L0_ffn_proj2_bias, L0_ffn_gate_w):
    import numpy as np
    import concourse.bacc as bacc
    from concourse.bass_utils import run_bass_kernel_spmd

    def tiles(w):
        k, n = w.shape
        return w.reshape(k // P, P, n).transpose(1, 0, 2).reshape(P, -1)

    wq = np.asarray(L0_attn_Wq).reshape(DIM, HEADS, DQK)
    wq = np.concatenate([wq[:, :, :DH].reshape(DIM, -1), wq[:, :, DH:].reshape(DIM, -1)], axis=1)
    wkr = np.asarray(L0_attn_Wkr)
    wkr = np.concatenate([wkr, wkr[:, ROPE // 2:], wkr[:, :ROPE // 2]], axis=1)
    wukv = np.asarray(L0_attn_Wukv).reshape(LATENT, HEADS, 2 * DH)
    weights = np.concatenate([tiles(wq), tiles(np.asarray(L0_attn_Wdkv)), tiles(wkr),
                              wukv[:, :, :DH].reshape(LATENT, -1), wukv[:, :, DH:].reshape(LATENT, -1),
                              tiles(np.asarray(L0_attn_Wo))], axis=1)

    inv_freq = (1.0 / 10000.0 ** (np.arange(0, ROPE, 2, dtype=np.float32) / ROPE)).astype(np.float32)
    angle = np.arange(SEQ, dtype=np.float32)[:, None] * inv_freq[None, :]
    cos = np.cos(np.concatenate([angle, angle], 1)).astype(np.float32)
    sin = np.sin(np.concatenate([-angle, angle], 1)).astype(np.float32)
    rope_tok = np.stack([cos, sin]).reshape(2, TT, P, ROPE).transpose(2, 0, 1, 3)
    rope_feat = np.concatenate([cos.T, sin.T], axis=0)
    diagonal = np.where(np.tril(np.ones((P, P), bool)), 0.0, MASKED).astype(np.float32)
    causal = np.concatenate([diagonal, np.zeros((P, P), np.float32), diagonal], axis=1)

    arrays = {
        "c_parts": np.asarray(x).transpose(3, 2, 1, 0),
        "log_dt": np.asarray(L0_tok_log_dt),
        "log_w_real": np.asarray(L0_tok_log_w_real).T,
        "w_imag": np.asarray(L0_tok_w_imag).T,
        "weights": weights,
        "rope_tok": rope_tok,
        "rope_feat": rope_feat,
        "causal": causal,
        "w_up": np.asarray(L0_ffn_proj1).reshape(HIDDEN // P, P, KD, P).transpose(3, 0, 2, 1).reshape(P, HIDDEN // P, DIM),
        "w_down": np.asarray(L0_ffn_proj2).reshape(DIM, HIDDEN // P, P).transpose(2, 1, 0),
        "bias_up": np.asarray(L0_ffn_proj1_bias).reshape(HIDDEN // P, P).T,
        "bias_down": np.asarray(L0_ffn_proj2_bias),
    }
    arrays = {k: np.ascontiguousarray(v) for k, v in arrays.items()}
    nc = bacc.Bacc("TRN2", target_bir_lowering=False, num_devices=1)
    args = [nc.dram_tensor(k, v.shape, mybir.dt.from_np(v.dtype), kind="ExternalInput").ap() for k, v in arrays.items()]
    out = nc.dram_tensor("out", (TOKENS, DIM), F32, kind="ExternalOutput").ap()
    vit_layer(nc, *args, out)
    r = run_bass_kernel_spmd(nc, [arrays], core_ids=[0])
    return r.results[0]["out"].reshape(BATCH, SEQ, DIM)
```
